# Optimizing a Trainium2 kernel written in Bass

```python
import numpy as np
import jax
import jax.numpy as jnp

def _softmax(x, axis=-1):
    return jax.nn.softmax(x, axis=axis)

def _gelu(x):
    return jax.nn.gelu(x, approximate=True)

def _silu(x):
    return jax.nn.silu(x)

def _sigmoid(x):
    return jax.nn.sigmoid(x)

def _layernorm(x, axis=-1, eps=1e-05):
    m = jnp.mean(x, axis=axis, keepdims=True)
    v = jnp.var(x, axis=axis, keepdims=True)
    return (x - m) / jnp.sqrt(v + eps)

def _scatter_add(tgt, idx, src, axis=0):
    return tgt.at[idx].add(src)

def _segment_sum(src, seg, n):
    return jax.ops.segment_sum(src, seg, n)
kernel_name = 'mk_hybrid_d1_jaxref_r8_2f8aec'

def setup_inputs(seed: int=0):
    np.random.seed(seed)
    _w = jnp.asarray

    def _L0_attn_a_setup():
        import jax, jax.numpy as jnp
        import numpy as np
        D_MODEL = 128
        NHEAD = 16
        HEAD_DIM = D_MODEL // NHEAD
        SCALE = HEAD_DIM ** (-0.5)
        EPS_LN = 1e-05
        key = jax.random.key(seed)
        ks = jax.random.split(key, 7)
        B, T, D = (2, 256, D_MODEL)
        x = jax.random.normal(ks[0], (B, T, D), dtype=jnp.float32)
        ln_gamma = jnp.ones((D,), dtype=jnp.float32)
        ln_beta = jnp.zeros((D,), dtype=jnp.float32)
        s = 1.0 / np.sqrt(D)
        W_qkv = jax.random.uniform(ks[1], (D, 3 * D), minval=-s, maxval=s, dtype=jnp.float32)
        b_qkv = jax.random.uniform(ks[2], (3 * D,), minval=-s, maxval=s, dtype=jnp.float32)
        W_proj = jax.random.uniform(ks[3], (D, D), minval=-s, maxval=s, dtype=jnp.float32)
        b_proj = jax.random.uniform(ks[4], (D,), minval=-s, maxval=s, dtype=jnp.float32)
        return {'x': x, 'ln_gamma': ln_gamma, 'ln_beta': ln_beta, 'W_qkv': W_qkv, 'b_qkv': b_qkv, 'W_proj': W_proj, 'b_proj': b_proj}
    _L0_attn_a_in = _L0_attn_a_setup()

    def _L0_attn_b_setup():
        import jax, jax.numpy as jnp
        import numpy as np
        NUM_HEADS = 16
        SUMMARY_COLS = 1

        def _masks(seq_len: int, stride: int, summary_cols: int):
            i = jnp.arange(seq_len)[:, None]
            j = jnp.arange(seq_len)[None, :]
            causal = j <= i
            strided = causal & ((i - j < stride) | (j % stride == i % stride))
            fixed = causal & ((j // stride == i // stride) | (j % stride >= max(0, stride - summary_cols)))
            return (strided, fixed)
        key = jax.random.key(seed)
        ks = jax.random.split(key, 5)
        B, S, H = (2, 256, 128)
        x = jax.random.normal(ks[0], (B, S, H), dtype=jnp.float32)
        scale = 1.0 / np.sqrt(H)
        Wq = jax.random.normal(ks[1], (H, H), dtype=jnp.float32) * scale
        Wk = jax.random.normal(ks[2], (H, H), dtype=jnp.float32) * scale
        Wv = jax.random.normal(ks[3], (H, H), dtype=jnp.float32) * scale
        Wo = jax.random.normal(ks[4], (H, H), dtype=jnp.float32) * scale
        return {'x': x, 'Wq': Wq, 'Wk': Wk, 'Wv': Wv, 'Wo': Wo}
    _L0_attn_b_in = _L0_attn_b_setup()

    def _L0_ffn_setup():
        import jax, jax.numpy as jnp
        import numpy as np
        D_MODEL = 128
        FFN_DIM = 256
        NUM_EXPERTS = 8
        NUM_GROUPS = 4
        EXPERTS_PER_GROUP = NUM_EXPERTS // NUM_GROUPS
        TOP_K = 2
        GROUPS_TOP_K = 1
        EPS = 1e-09

        def _topk_normalized(scores, k):
            vals, idx = jax.lax.top_k(scores, k)
            vals = vals / (jnp.sum(vals, axis=-1, keepdims=True) + EPS)
            return (vals, idx)
        key = jax.random.key(seed)
        ks = jax.random.split(key, 6)
        B, S = (2, 128)
        x = jax.random.normal(ks[0], (B, S, D_MODEL), dtype=jnp.float32)
        sd = 0.02
        macro_w = jax.random.normal(ks[1], (D_MODEL, NUM_GROUPS), dtype=jnp.float32) * sd
        micro_w = jax.random.normal(ks[2], (NUM_GROUPS, D_MODEL, EXPERTS_PER_GROUP), dtype=jnp.float32) * sd
        gate_w = jax.random.normal(ks[3], (NUM_EXPERTS, D_MODEL, FFN_DIM), dtype=jnp.float32) * sd
        up_w = jax.random.normal(ks[4], (NUM_EXPERTS, D_MODEL, FFN_DIM), dtype=jnp.float32) * sd
        down_w = jax.random.normal(ks[5], (NUM_EXPERTS, FFN_DIM, D_MODEL), dtype=jnp.float32) * sd
        return {'x': x, 'macro_w': macro_w, 'micro_w': micro_w, 'gate_w': gate_w, 'up_w': up_w, 'down_w': down_w}
    _L0_ffn_in = _L0_ffn_setup()
    _d = {'L0_attn_a_x': _L0_attn_a_in['x'], 'L0_attn_a_ln_gamma': _L0_attn_a_in['ln_gamma'], 'L0_attn_a_ln_beta': _L0_attn_a_in['ln_beta'], 'L0_attn_a_W_qkv': _L0_attn_a_in['W_qkv'], 'L0_attn_a_b_qkv': _L0_attn_a_in['b_qkv'], 'L0_attn_a_W_proj': _L0_attn_a_in['W_proj'], 'L0_attn_a_b_proj': _L0_attn_a_in['b_proj'], 'L0_attn_b_Wq': _L0_attn_b_in['Wq'], 'L0_attn_b_Wk': _L0_attn_b_in['Wk'], 'L0_attn_b_Wv': _L0_attn_b_in['Wv'], 'L0_attn_b_Wo': _L0_attn_b_in['Wo'], 'L0_ffn_macro_w': _L0_ffn_in['macro_w'], 'L0_ffn_micro_w': _L0_ffn_in['micro_w'], 'L0_ffn_gate_w': _L0_ffn_in['gate_w'], 'L0_ffn_up_w': _L0_ffn_in['up_w'], 'L0_ffn_down_w': _L0_ffn_in['down_w']}
    _x0 = _d['L0_attn_a_x']
    _d['L0_attn_a_x'] = jax.random.normal(jax.random.fold_in(jax.random.key(seed), 1), (16, 512, 128), dtype=_x0.dtype)
    del _x0
    return _d

def reference(L0_attn_a_x, L0_attn_a_ln_gamma, L0_attn_a_ln_beta, L0_attn_a_W_qkv, L0_attn_a_b_qkv, L0_attn_a_W_proj, L0_attn_a_b_proj, L0_attn_b_Wq, L0_attn_b_Wk, L0_attn_b_Wv, L0_attn_b_Wo, L0_ffn_macro_w, L0_ffn_micro_w, L0_ffn_gate_w, L0_ffn_up_w, L0_ffn_down_w):

    def _L0_attn_a_ref(x, ln_gamma, ln_beta, W_qkv, b_qkv, W_proj, b_proj):
        import jax, jax.numpy as jnp
        import numpy as np
        D_MODEL = 128
        NHEAD = 16
        HEAD_DIM = D_MODEL // NHEAD
        SCALE = HEAD_DIM ** (-0.5)
        EPS_LN = 1e-05
        B, T, D = x.shape
        h, dh = (NHEAD, HEAD_DIM)
        mu = jnp.mean(x, axis=-1, keepdims=True)
        var = jnp.mean(jnp.square(x - mu), axis=-1, keepdims=True)
        x_n = (x - mu) * jax.lax.rsqrt(var + EPS_LN) * ln_gamma + ln_beta
        qkv = x_n @ W_qkv + b_qkv
        q, k, v = jnp.split(qkv, 3, axis=-1)
        q = q.reshape(B, T, h, dh).transpose(0, 2, 1, 3)
        k = k.reshape(B, T, h, dh).transpose(0, 2, 1, 3)
        v = v.reshape(B, T, h, dh).transpose(0, 2, 1, 3)
        scores = jnp.einsum('bhqd,bhkd->bhqk', q, k) * SCALE
        scores = scores - jnp.max(scores, axis=-1, keepdims=True)
        attn = jnp.exp(scores)
        attn = attn / jnp.maximum(jnp.sum(attn, axis=-1, keepdims=True), 1e-12)
        ctx = jnp.einsum('bhqk,bhkd->bhqd', attn, v)
        ctx = ctx.transpose(0, 2, 1, 3).reshape(B, T, D)
        return ctx @ W_proj + b_proj

    def _L0_attn_b_ref(x, Wq, Wk, Wv, Wo):
        import jax, jax.numpy as jnp
        import numpy as np
        NUM_HEADS = 16
        SUMMARY_COLS = 1

        def _masks(seq_len: int, stride: int, summary_cols: int):
            i = jnp.arange(seq_len)[:, None]
            j = jnp.arange(seq_len)[None, :]
            causal = j <= i
            strided = causal & ((i - j < stride) | (j % stride == i % stride))
            fixed = causal & ((j // stride == i // stride) | (j % stride >= max(0, stride - summary_cols)))
            return (strided, fixed)
        B, S, H = x.shape
        nh = NUM_HEADS
        hd = H // nh
        scale = hd ** (-0.5)
        stride = max(1, int(np.sqrt(S)))

        def split_heads(t):
            return t.reshape(B, S, nh, hd).transpose(0, 2, 1, 3)
        q = split_heads(x @ Wq.T)
        k = split_heads(x @ Wk.T)
        v = split_heads(x @ Wv.T)
        scores = jnp.einsum('bhqd,bhkd->bhqk', q, k) * scale
        strided, fixed = _masks(S, stride, SUMMARY_COLS)
        half = max(1, nh // 2)
        head_mask = jnp.concatenate([jnp.broadcast_to(strided, (half, S, S)), jnp.broadcast_to(fixed, (nh - half, S, S))], axis=0)
        neg_inf = jnp.finfo(scores.dtype).min
        scores = jnp.where(head_mask[None], scores, neg_inf)
        attn = jax.nn.softmax(scores, axis=-1)
        out = jnp.einsum('bhqk,bhkd->bhqd', attn, v)
        out = out.transpose(0, 2, 1, 3).reshape(B, S, H)
        return out @ Wo.T

    def _L0_ffn_ref(x, macro_w, micro_w, gate_w, up_w, down_w):
        import jax, jax.numpy as jnp
        import numpy as np
        D_MODEL = 128
        FFN_DIM = 256
        NUM_EXPERTS = 8
        NUM_GROUPS = 4
        EXPERTS_PER_GROUP = NUM_EXPERTS // NUM_GROUPS
        TOP_K = 2
        GROUPS_TOP_K = 1
        EPS = 1e-09

        def _topk_normalized(scores, k):
            vals, idx = jax.lax.top_k(scores, k)
            vals = vals / (jnp.sum(vals, axis=-1, keepdims=True) + EPS)
            return (vals, idx)
        B, S, D = x.shape
        T = B * S
        xf = x.reshape(T, D)
        macro_scores = jax.nn.sigmoid(xf @ macro_w)
        mv, mi = _topk_normalized(macro_scores, GROUPS_TOP_K)
        macro_full = jnp.sum(jax.nn.one_hot(mi, NUM_GROUPS, dtype=xf.dtype) * mv[..., None], axis=1)
        micro_scores = jax.nn.sigmoid(jnp.einsum('td,gde->tge', xf, micro_w))
        uv, ui = _topk_normalized(micro_scores, TOP_K)
        micro_full = jnp.sum(jax.nn.one_hot(ui, EXPERTS_PER_GROUP, dtype=xf.dtype) * uv[..., None], axis=2)
        w = (macro_full[:, :, None] * micro_full).reshape(T, NUM_EXPERTS)
        gate = jax.nn.silu(jnp.einsum('td,edf->tef', xf, gate_w))
        up = jnp.einsum('td,edf->tef', xf, up_w)
        h = gate * up
        out = jnp.einsum('te,tef,efd->td', w, h, down_w)
        return out.reshape(B, S, D)
    x = L0_attn_a_x
    x = x + _L0_attn_a_ref(_layernorm(x, axis=-1), L0_attn_a_ln_gamma, L0_attn_a_ln_beta, L0_attn_a_W_qkv, L0_attn_a_b_qkv, L0_attn_a_W_proj, L0_attn_a_b_proj)
    x = x + _L0_ffn_ref(_layernorm(x, axis=-1), L0_ffn_macro_w, L0_ffn_micro_w, L0_ffn_gate_w, L0_ffn_up_w, L0_ffn_down_w)
    x = x + _L0_attn_b_ref(_layernorm(x, axis=-1), L0_attn_b_Wq, L0_attn_b_Wk, L0_attn_b_Wv, L0_attn_b_Wo)
    x = x + _L0_ffn_ref(_layernorm(x, axis=-1), L0_ffn_macro_w, L0_ffn_micro_w, L0_ffn_gate_w, L0_ffn_up_w, L0_ffn_down_w)
    return x

_drawn_inputs = setup_inputs


def setup_inputs(seed=0):
    import zlib

    import numpy as np

    out = dict(_drawn_inputs(seed))
    spreads = {'L0_attn_a_ln_gamma': (1.0, 0.6), 'L0_attn_a_ln_beta': (0.0, 0.1)}
    factors = {'L0_ffn_macro_w': 6.157,
     'L0_ffn_micro_w': 8.0,
     'L0_ffn_gate_w': 5.28,
     'L0_ffn_up_w': 5.253,
     'L0_ffn_down_w': 5.241}
    for name, (base, spread) in spreads.items():
        noise = np.random.default_rng([zlib.crc32(name.encode()), seed]).standard_normal(out[name].shape)
        drawn = base * np.exp(spread * noise) if base else spread * noise
        out[name] = jnp.asarray(drawn.astype(out[name].dtype))
    for name, factor in factors.items():
        out[name] = (out[name] * factor).astype(out[name].dtype)
    return out
```

```python
from contextlib import ExitStack

import concourse.bass as bass
from concourse import mybir

P = 128
NB, SEQ, D = 16, 512, 128
HEADS, HD = 16, 8
TPB = SEQ // P
NT = NB * TPB
HG = 4
NG = NB * HEADS // HG
VW = P // HG
EXPERTS, FF, RG = 8, 256, 4
EPG = EXPERTS // RG
GUW = EPG * 2 * FF
DNC = EPG * FF // P
SLOTS = NT + RG
ROW = D + EPG
SCALE = HD ** -0.5
EPS_LN, EPS_TOPK, EPS_DEN = 1e-5, 1e-9, 1e-12
REPEATS = [3, 2, 1]
MROW = 64

F32, BF16, I32, U32 = mybir.dt.float32, mybir.dt.bfloat16, mybir.dt.int32, mybir.dt.uint32
ALU = mybir.AluOpType
ACT = mybir.ActivationFunctionType
AX = mybir.AxisListType


def wait(eng, sem, value):
    if not isinstance(value, int) or value > 0:
        eng.wait_ge(sem, value)


def in_turns(eng, step, rounds, buffers):
    for u in range(buffers):
        step(0, u)
    with eng.Fori(1, rounds) as i:
        for u in range(buffers):
            step(i, u)


def one_ahead(eng, front, back, rounds):
    front(0, 0)
    front(0, 1)
    back(0, 0)
    front(1, 0)
    back(0, 1)
    with eng.Fori(1, rounds - 1) as i:
        for u in range(2):
            front(i + u, 1 - u)
            back(i, u)
    front(rounds - 1, 1)
    back(rounds - 1, 0)
    back(rounds - 1, 1)


class Phase:

    own_sems = []

    def __init__(self, nc, name):
        self.nc, self.name, self.ctx = nc, name, ExitStack()
        self.used, self.blocks = [], []

    def __enter__(self):
        self.ctx.__enter__()
        return self

    def __exit__(self, *a):
        if self.blocks:
            self.blocks.pop().__exit__(*a)
            if self.used and a[0] is None:
                with self.nc.Block() as clear:
                    @clear.sync
                    def _(sp):
                        for sem in self.used:
                            sp.sem_clear(sem)
        return self.ctx.__exit__(*a)

    def sb(self, name, shape, dt):
        return self.ctx.enter_context(self.nc.sbuf_tensor(f"{self.name}_{name}", shape, dt))

    def ps(self, name, shape, dt=F32):
        return self.ctx.enter_context(self.nc.psum_tensor(f"{self.name}_{name}", shape, dt))

    def sem(self, name):
        self.used.append(self.ctx.enter_context(self.nc.semaphore(f"{self.name}_{name}")))
        return self.used[-1]

    def software_sems(self, n):
        return [self.own_sems.pop() for _ in range(n)]

    def sems(self, name, n):
        return [self.sem(f"{name}{i}") for i in range(n)]

    def block(self):
        self.blocks.append(self.nc.Block())
        return self.blocks[-1].__enter__()


def load_constants(nc, name, loads):
    with Phase(nc, name) as ph:
        landed = ph.sem("landed")
        block = ph.block()

        @block.sync
        def _(sp):
            for dst, src in loads:
                sp.dma_start(dst, src).then_inc(landed, 16)
            sp.wait_ge(landed, 16 * len(loads))


def finish_stats(nc, name, stats, mean, rstd, twice):
    with Phase(nc, name) as ph:
        tmp = ph.sb("tmp", [P, NT], F32)
        var = ph.sb("var", [P, NT], F32)
        inner = ph.sb("inner", [P, 2, NT], F32)
        dve_step, var_ready, std_ready = ph.sem("dve_step"), ph.sem("var_ready"), ph.sem("std_ready")
        block = ph.block()

        @block.vector
        def _(dve):
            dve.tensor_tensor(tmp[:], stats[:, :, 1], stats[:, :, 4], ALU.subtract)
            dve.tensor_tensor(var[:], stats[:, :, 2], stats[:, :, 5], ALU.add)
            dve.tensor_tensor(mean[:], stats[:, :, 1], stats[:, :, 4], ALU.add).then_inc(dve_step, 1)
            dve.wait_ge(dve_step, 1)
            dve.tensor_tensor(tmp[:], tmp[:], tmp[:], ALU.mult)
            dve.tensor_scalar(var[:], var[:], 1.0 / D, None, ALU.mult)
            dve.tensor_scalar(mean[:], mean[:], 0.5, None, ALU.mult).then_inc(dve_step, 1)
            dve.wait_ge(dve_step, 2)
            dve.scalar_tensor_tensor(inner[:, 0], tmp[:], 0.25, var[:], ALU.mult, ALU.add).then_inc(dve_step, 1)
            dve.wait_ge(dve_step, 3)
            dve.tensor_scalar(var[:], inner[:, 0], EPS_LN, None, ALU.add).then_inc(var_ready, 1)
            dve.wait_ge(std_ready, 1)
            dve.reciprocal(rstd[:], tmp[:]).then_inc(dve_step, 1)
            if twice:
                dve.wait_ge(dve_step, 4)
                dve.tensor_tensor(inner[:, 1], rstd[:], rstd[:], ALU.mult).then_inc(dve_step, 1)
                dve.wait_ge(dve_step, 5)
                dve.tensor_tensor(inner[:, 0], inner[:, 0], inner[:, 1], ALU.mult).then_inc(dve_step, 1)
                dve.wait_ge(dve_step, 6)
                dve.tensor_scalar(var[:], inner[:, 0], EPS_LN, None, ALU.add).then_inc(var_ready, 1)
                dve.wait_ge(std_ready, 2)
                dve.reciprocal(inner[:, 1], tmp[:]).then_inc(dve_step, 1)
                dve.wait_ge(dve_step, 7)
                dve.tensor_tensor(rstd[:], rstd[:], inner[:, 1], ALU.mult)

        @block.scalar
        def _(act):
            for n in range(2 if twice else 1):
                act.wait_ge(var_ready, n + 1)
                act.activation(tmp[:], var[:], ACT.Sqrt).then_inc(std_ready, 1)


def project(nc, name, src, mean, rstd, w, scratch, identity):
    q_parts, k_parts, v_strips = scratch
    with Phase(nc, name) as ph:
        xn = ph.sb("xn", [P, 2, TPB, D], F32)
        xT = ph.sb("xT", [P, 2, SEQ], F32)
        parts = ph.sb("parts", [P, 2, 2, 3, SEQ], BF16)
        rest = ph.sb("rest", [P, 2, 2, SEQ], F32)
        strips = ph.sb("strips", [P, 2, TPB, HEADS, VW], F32)
        scaled = ph.sb("scaled", [P, P + 1], F32)
        p_xT = ph.ps("p_xT", [P, 2, SEQ])
        p_qk = ph.ps("p_qk", [P, 2, 2, SEQ])
        p_v = ph.ps("p_v", [P, 2, SEQ])
        setup = ph.sem("setup")
        xn_ready, xT_done, xT_ready = (ph.sems(n, 2) for n in ("xn_ready", "xT_done", "xT_ready"))
        qk_ready, v_ready = ph.sems("qk_ready", 2), ph.sems("v_ready", 2)
        hi_ready, rest_ready = ph.sems("hi_ready", 2), ph.sems("rest_ready", 2)
        mid_ready, lo_ready, v_copied = ph.sems("mid_ready", 2), ph.sems("lo_ready", 2), ph.sems("v_copied", 2)
        stored = ph.sems("stored", 2)
        n_stores = 6 + TPB
        block = ph.block()

        @block.vector
        def _(dve):
            dve.memset(strips[:], 1.0)
            dve.tensor_scalar(scaled[:, 0:P], w["q"][:], SCALE, None, ALU.mult)
            dve.tensor_scalar(scaled[:, P:P + 1], w["bq"][:], SCALE, None, ALU.mult).then_inc(setup, 1)
            dve.wait_ge(setup, 1)
            def front(i, u):
                b = 2 * i + u
                wait(dve, xT_done[u], i)
                for t in range(TPB):
                    tile = TPB * b + t
                    last = dve.tensor_scalar(xn[:, u, t, :], src[:, tile, :], mean[:, bass.ds(tile, 1)],
                                             rstd[:, bass.ds(tile, 1)], ALU.subtract, ALU.mult)
                last.then_inc(xn_ready[u], 1)

            def back(i, u):
                wait(dve, stored[u], 16 * n_stores * i)
                for z in range(2):
                    bias = scaled[:, P:P + 1] if z == 0 else w["bk"][:]
                    dve.wait_ge(hi_ready[u], 2 * i + z + 1)
                    wait(dve, lo_ready[u], 2 * i)
                    dve.scalar_tensor_tensor(rest[:, u, z, :], p_qk[:, u, z, :], bias, parts[:, u, z, 0, :],
                                             ALU.add, ALU.subtract).then_inc(rest_ready[u], 1)
                    dve.wait_ge(rest_ready[u], 2 * i + z + 1)
                    dve.tensor_copy(parts[:, u, z, 1, :], rest[:, u, z, :]).then_inc(mid_ready[u], 1)
                dve.wait_ge(v_ready[u], i + 1)
                dve.tensor_tensor(strips[:, u, :, :, 0:HD],
                                  p_v[:, u, :].rearrange("p (t h d) -> p t h d", t=TPB, h=HEADS),
                                  w["bv"][:].rearrange("p (o h d) -> p o h d", o=1, h=HEADS)
                                  .to_broadcast([P, TPB, HEADS, HD]), ALU.add).then_inc(v_copied[u], 1)

            one_ahead(dve, front, back, NB // 2)

        @block.scalar
        def _(act):
            act.wait_ge(setup, 1)
            def front(i, u):
                act.wait_ge(xT_done[u], i + 1)
                wait(act, v_ready[u], i)
                act.activation(xT[:, u, :], p_xT[:, u, :], ACT.Identity, scale=w["gamma"][:],
                               bias=w["beta"][:]).then_inc(xT_ready[u], 1)

            def back(i, u):
                wait(act, stored[u], 16 * n_stores * i)
                for z in range(2):
                    bias = scaled[:, P:P + 1] if z == 0 else w["bk"][:]
                    act.wait_ge(qk_ready[u], 2 * i + z + 1)
                    act.activation(parts[:, u, z, 0, :], p_qk[:, u, z, :], ACT.Identity,
                                   bias=bias).then_inc(hi_ready[u], 1)

            one_ahead(act, front, back, NB // 2)

        @block.gpsimd
        def _(pool):
            def step(i, u):
                wait(pool, stored[u], 16 * n_stores * i)
                for z in range(2):
                    pool.wait_ge(mid_ready[u], 2 * i + z + 1)
                    pool.tensor_tensor(parts[:, u, z, 2, :], rest[:, u, z, :], parts[:, u, z, 1, :],
                                       ALU.subtract).then_inc(lo_ready[u], 1)

            in_turns(pool, step, NB // 2, 2)

        @block.tensor
        def _(pe):
            pe.wait_ge(setup, 1)
            def front(i, u):
                pe.wait_ge(xn_ready[u], i + 1)
                wait(pe, xT_ready[u], i)
                for t in range(TPB):
                    last = pe.transpose(p_xT[:, u, t * P:(t + 1) * P], xn[:, u, t, :], identity[:])
                last.then_inc(xT_done[u], 1)

            def back(i, u):
                pe.wait_ge(xT_ready[u], i + 1)
                wait(pe, rest_ready[u], 2 * i)
                pe.matmul(p_qk[:, u, 0, :], scaled[:, 0:P], xT[:, u, :], start=True, stop=True)\
                    .then_inc(qk_ready[u], 1)
                pe.matmul(p_qk[:, u, 1, :], w["k"][:], xT[:, u, :], start=True, stop=True)\
                    .then_inc(qk_ready[u], 1)
                wait(pe, v_copied[u], i)
                for t in range(TPB):
                    last = pe.matmul(p_v[:, u, t * P:(t + 1) * P], xT[:, u, t * P:(t + 1) * P], w["v"][:],
                                     start=True, stop=True)
                last.then_inc(v_ready[u], 1)

            one_ahead(pe, front, back, NB // 2)

        @block.sync
        def _(sp):
            q_by_seq = q_parts.rearrange("s (b g) r t -> s b (g r) t", g=HG)
            k_by_seq = k_parts.rearrange("s (b g) r t -> s b (g r) t", g=HG)
            v_by_seq = v_strips.rearrange("(b g) p t c -> b g p t c", g=HG)
            def step(i, u):
                b = 2 * i + u
                for z, dst in ((0, q_by_seq), (1, k_by_seq)):
                    sp.wait_ge(lo_ready[u], 2 * i + z + 1)
                    for s in range(3):
                        sp.dma_start(dst[s, b], parts[:, u, z, s, :]).then_inc(stored[u], 16)
                sp.wait_ge(v_copied[u], i + 1)
                for g in range(HG):
                    sp.dma_start(v_by_seq[b, g],
                                 strips[:, u, :, g * HG:(g + 1) * HG, :].rearrange("p t j c -> p t (j c)"))\
                        .then_inc(stored[u], 16)

            in_turns(sp, step, NB // 2, 2)
            for u in range(2):
                sp.wait_ge(stored[u], 16 * n_stores * (NB // 2))


def attend(nc, name, scratch, ctx_out, identity, identity_bf, masks):
    q_parts, k_parts, v_strips = scratch
    causal = masks is not None
    with Phase(nc, name) as ph:
        NBUF, NP = 4, 8
        qs = [ph.sb(f"qs{v}", [P, HG, SEQ], BF16) for v in range(NBUF)]
        ks = [ph.sb(f"ks{v}", [P, HG, SEQ], BF16) for v in range(NBUF)]
        vs = [ph.sb(f"vs{v}", [P, TPB, HG, VW], F32) for v in range(NBUF)]
        zeros = ph.sb("zeros", [3, HG * SEQ], BF16)
        neg_max = ph.sb("neg_max", [P, NBUF, HG * TPB], F32)
        max_rest = ph.sb("max_rest", [P, NBUF, HG * TPB], F32)
        max_parts = ph.sb("max_parts", [P, NBUF, P], BF16)
        none = ph.sb("none", [P, HG * TPB], F32)
        max_rows = ph.sb("max_rows", [P, NBUF, P], BF16)
        probs = ph.sb("probs", [P, NP, SEQ], F32)
        ctx_sb = ph.sb("ctx_sb", [P, SEQ], F32)
        den = ph.sb("den", [P, 2, TPB, HG], F32)
        p_max = ph.ps("p_max", [P, 2, 2, SEQ])
        p_sc = ph.ps("p_sc", [P, 2, SEQ])
        p_ctx = ph.ps("p_ctx", [P, SEQ])
        p_tr = ph.ps("p_tr", [P, SEQ])
        p_tr_bf = p_tr[:].bitcast(BF16)
        setup = ph.sem("setup")
        loaded = ph.sems("loaded", NBUF)
        max_landed = ph.sems("max_landed", NBUF)
        max_scores, max_done = ph.sem("max_scores"), ph.sem("max_done")
        split_step, split_done = ph.sem("split_step"), ph.sem("split_done")
        rows_ready, rows_copied = ph.sem("rows_ready"), ph.sem("rows_copied")
        scores, exps, products = ph.sem("scores"), ph.sem("exps"), ph.sem("products")
        ctx_copied, ctx_turned, normalised = ph.sem("ctx_copied"), ph.sem("ctx_turned"), ph.sem("normalised")
        norm_step = ph.sem("norm_step")
        LOADS = 2 * sum(REPEATS) + 2
        UNITS = TPB * HG
        MAXU = 2 * HG
        block = ph.block()

        def at(k, c, m=0):
            return 4 * k + c + m, (c + m) % NBUF, k + (c + m) // NBUF

        def pipeline(eng, step, first=-3, last=NG):
            for n in range(first, 5):
                step(0, n)
            with eng.Fori(1, NB - 1) as k:
                for c in range(1, 5):
                    step(k, c)
            for n in range(NG - 3, last + 1):
                step(0, n)

        def inside(k, c, m):
            return not isinstance(k, int) or 0 <= 4 * k + c + m < NG

        @block.vector
        def _(dve):
            for v in range(NBUF):
                dve.memset(qs[v][:], 0.0)
                dve.memset(ks[v][:], 0.0)
            dve.memset(zeros[:], 0.0)
            dve.memset(max_parts[:], 0.0)
            dve.memset(none[:], 0.0).then_inc(setup, 1)
            dve.wait_ge(setup, 1)
            for v in range(NBUF):
                last = dve.memset(ks[v][MROW:MROW + 3, :, :], 1.0)
            last.then_inc(setup, 1)

            def reduce_unit(k, c, m):
                n, v, _ = at(k, c, 2)
                j, half = m // 2, m % 2
                width = P * (2 * half + 2) if causal else SEQ
                dve.wait_ge(max_scores, MAXU * n + m + 1)
                dve.tensor_reduce(neg_max[:, v, TPB * j + 2 * half:TPB * j + 2 * half + 2],
                                  p_max[:, m % 2, :, 0:width], AX.X, ALU.max, negate=True).then_inc(max_done, 1)

            def normalise(k, c):
                n, v, use = at(k, c, -1)
                turned = p_tr[:].rearrange("p (t j w) -> p t j w", t=TPB, j=HG)
                dve.wait_ge(ctx_turned, n + 1)
                dve.tensor_scalar(den[:, 0], turned[:, :, :, HD], EPS_DEN, None, ALU.max).then_inc(norm_step, 1)
                dve.wait_ge(norm_step, 2 * n + 1)
                dve.reciprocal(den[:, 1], den[:, 0]).then_inc(norm_step, 1)
                dve.wait_ge(norm_step, 2 * n + 2)
                dst = ctx_out[:].rearrange("p (b t) c -> p b t c", t=TPB)[:, use, :, v * HG * HD:(v + 1) * HG * HD]
                dve.tensor_tensor(dst.rearrange("p t (j d) -> p t j d", j=HG), turned[:, :, :, 0:HD],
                                  den[:, 1].rearrange("p t (j o) -> p t j o", o=1)
                                  .to_broadcast([P, TPB, HG, HD]), ALU.mult).then_inc(normalised, 1)

            def step(k, c):
                for m in range(MAXU):
                    if inside(k, c, 2):
                        reduce_unit(k, c, m)
                    if m == 5 and inside(k, c, -1):
                        normalise(k, c)

            pipeline(dve, step, first=-2)

        @block.gpsimd
        def _(pool):
            pool.wait_ge(setup, 1)

            def step(k, c):
                if not inside(k, c, 2):
                    return
                n, v, _ = at(k, c, 2)
                part = [max_parts[:, v, s * HG * TPB:(s + 1) * HG * TPB] for s in range(3)]
                pool.wait_ge(max_done, MAXU * (n + 1))
                pool.tensor_tensor(part[0], neg_max[:, v, :], none[:], ALU.subtract).then_inc(split_step, 1)
                pool.wait_ge(split_step, 4 * n + 1)
                pool.tensor_tensor(max_rest[:, v, :], neg_max[:, v, :], part[0], ALU.subtract)\
                    .then_inc(split_step, 1)
                pool.wait_ge(split_step, 4 * n + 2)
                pool.tensor_tensor(part[1], max_rest[:, v, :], none[:], ALU.subtract).then_inc(split_step, 1)
                pool.wait_ge(split_step, 4 * n + 3)
                pool.tensor_tensor(part[2], max_rest[:, v, :], part[1], ALU.subtract)\
                    .then_inc(split_step, 1)

            pipeline(pool, step, first=-2)

        @block.scalar
        def _(act):
            def copy_rows(k, c):
                n, v, _ = at(k, c, 1)
                act.wait_ge(rows_ready, n + 1)
                act.copy(max_rows[:, v, :], p_tr_bf[:, 0:P]).then_inc(rows_copied, 1)

            def copy_ctx(k, c):
                n, _, _ = at(k, c, -1)
                act.wait_ge(products, TPB * (n + 1))
                wait(act, ctx_turned, n)
                act.copy(ctx_sb[:], p_ctx[:]).then_inc(ctx_copied, 1)

            def step(k, c):
                n, _, _ = at(k, c)
                for s in range(UNITS):
                    if inside(k, c, 0):
                        kt = s // HG
                        first = P * kt if causal else 0
                        act.wait_ge(scores, UNITS * n + s + 1)
                        if s % HG == 0:
                            wait(act, products, TPB * n + kt - 1)
                        act.activation(probs[:, s % NP, first:SEQ], p_sc[:, s % 2, first:SEQ], ACT.Exp)\
                            .then_inc(exps, 1)
                    if s == 5 and inside(k, c, 1):
                        copy_rows(k, c)
                    if s == 4 and inside(k, c, -1):
                        copy_ctx(k, c)

            pipeline(act, step, first=-1)

        @block.tensor
        def _(pe):
            def max_unit(k, c, m):
                n, v, use = at(k, c, 2)
                j, half = m // 2, m % 2
                width = P * (2 * half + 2) if causal else SEQ
                if m == 0:
                    pe.wait_ge(loaded[v], 16 * LOADS * (use + 1))
                wait(pe, max_done, MAXU * n + m - 1)
                for r in range(2):
                    qt = 2 * half + r
                    last = pe.matmul(p_max[:, m % 2, r, 0:width], qs[v][:, j, qt * P:(qt + 1) * P],
                                     ks[v][:, j, 0:width], start=True, stop=not causal)
                    if causal:
                        last = pe.matmul(p_max[:, m % 2, r, 0:width], identity_bf[:],
                                         masks[:, v // 2, 0, qt, 0:width], start=False, stop=True)
                last.then_inc(max_scores, 1)

            def score_unit(k, c, s):
                n, v, use = at(k, c)
                kt, j = s // HG, s % HG
                first = P * kt if causal else 0
                if s == 0:
                    pe.wait_ge(max_landed[v], 16 * 3 * (use + 1))
                wait(pe, exps, UNITS * n + s - 1)
                last = pe.matmul(p_sc[:, s % 2, first:SEQ], ks[v][:, j, kt * P:(kt + 1) * P],
                                 qs[v][:, j, first:SEQ], start=True, stop=not causal)
                if causal:
                    last = pe.matmul(p_sc[:, s % 2, first:SEQ], identity_bf[:],
                                     masks[:, v // 2, 1, kt, first:SEQ], start=False, stop=True)
                last.then_inc(scores, 1)

            def value_products(k, c, kt, m=0):
                n, v, _ = at(k, c, m)
                first = P * kt if causal else 0
                pe.wait_ge(exps, UNITS * n + HG * (kt + 1))
                if kt == 0:
                    wait(pe, ctx_copied, n)
                for j in range(HG):
                    last = pe.matmul(p_ctx[VW * j:VW * (j + 1), first:SEQ], vs[v][:, kt, j, :],
                                     probs[:, (HG * kt + j) % NP, first:SEQ], start=(kt == 0), stop=(kt == TPB - 1))
                last.then_inc(products, 1)

            def turn_rows(k, c):
                n, v, _ = at(k, c, 1)
                pe.wait_ge(split_step, 4 * (n + 1))
                wait(pe, normalised, n - 2)
                pe.transpose(p_tr_bf[:, 0:P], max_parts[:, v, :], identity_bf[:]).then_inc(rows_ready, 1)

            def turn_ctx(k, c):
                n, _, _ = at(k, c, -1)
                pe.wait_ge(ctx_copied, n + 1)
                wait(pe, normalised, n)
                if inside(k, c, 1):
                    pe.wait_ge(rows_copied, n + 3)
                for t in range(TPB):
                    last = pe.transpose(p_tr[:, t * P:(t + 1) * P], ctx_sb[:, t * P:(t + 1) * P], identity[:])
                last.then_inc(ctx_turned, 1)

            pe.wait_ge(setup, 2)

            def step(k, c):
                for s in range(UNITS):
                    if inside(k, c, 0):
                        score_unit(k, c, s)
                    if s == 4 and inside(k, c, 1):
                        turn_rows(k, c)
                    if s % 2 == 1 and inside(k, c, 2):
                        max_unit(k, c, s // 2)
                    if s == 1 and inside(k, c, -1):
                        value_products(k, c, TPB - 1, -1)
                    if s in (6, 10, 14) and inside(k, c, 0):
                        value_products(k, c, (s - 6) // 4)
                    if s == 8 and inside(k, c, -1):
                        turn_ctx(k, c)

            pipeline(pe, step, first=-2)

        @block.sync
        def _(sp):
            def move_rows(k, c):
                n, v, _ = at(k, c, 1)
                sp.wait_ge(rows_copied, n + 1)
                for part in range(3):
                    sp.dma_start(qs[v][MROW + part:MROW + part + 1, :, :].rearrange("p j (t c) -> p (j t) c", c=P),
                                 max_rows[part * HG * TPB:(part + 1) * HG * TPB, v, :])\
                        .then_inc(max_landed[v], 16)

            def load(k, c):
                n, v, _ = at(k, c, 3)
                wait(sp, products, TPB * (n - 3))
                r = 0
                for part, times in enumerate(REPEATS):
                    for a in range(times):
                        rows = slice(HD * (r + a), HD * (r + a + 1))
                        sp.dma_start(qs[v][rows, :, :], q_parts[part, n].rearrange("(j d) t -> d j t", d=HD))\
                            .then_inc(loaded[v], 16)
                        sp.dma_start(ks[v][rows, :, :], k_parts[a, n].rearrange("(j d) t -> d j t", d=HD))\
                            .then_inc(loaded[v], 16)
                    r += times
                sp.dma_start(qs[v][MROW:MROW + 3, :, :].rearrange("p j t -> p (j t)"), zeros[:])\
                    .then_inc(loaded[v], 16)
                sp.dma_start(vs[v][:].rearrange("p t j c -> p t (j c)"), v_strips[n]).then_inc(loaded[v], 16)

            sp.wait_ge(setup, 2)

            def step(k, c):
                if inside(k, c, 3):
                    load(k, c)
                if inside(k, c, 1):
                    move_rows(k, c)

            pipeline(sp, step, first=-3)


def attention_out(nc, name, x, ctx_in, w, identity, stats):
    with Phase(nc, name) as ph:
        cx = ph.sb("cx", [P, 2, TPB, D], F32)
        cT = ph.sb("cT", [P, 2, SEQ], F32)
        y = ph.sb("y", [P, 2, TPB, D], F32)
        st = ph.sb("st", [P, 2, TPB, 6], F32)
        p_cT = ph.ps("p_cT", [P, 2, SEQ])
        p_y = ph.ps("p_y", [P, 2, TPB, D])
        copied, turned, cT_ready, y_ready, biased, added, kept, counted = (
            ph.sems(n, 2) for n in ("copied", "turned", "cT_ready", "y_ready", "biased", "added", "kept", "counted"))
        x_by_seq = x[:].rearrange("p (b t) d -> p b t d", t=TPB)
        ctx_by_seq = ctx_in[:].rearrange("p (b t) d -> p b t d", t=TPB)
        block = ph.block()

        @block.tensor
        def _(pe):
            def front(i, u):
                pe.wait_ge(copied[u], i + 1)
                wait(pe, cT_ready[u], i)
                for t in range(TPB):
                    last = pe.transpose(p_cT[:, u, t * P:(t + 1) * P], cx[:, u, t, :], identity[:])
                last.then_inc(turned[u], 1)

            def back(i, u):
                pe.wait_ge(cT_ready[u], i + 1)
                wait(pe, biased[u], i)
                for t in range(TPB):
                    last = pe.matmul(p_y[:, u, t, :], cT[:, u, t * P:(t + 1) * P], w["o"][:], start=True, stop=True)
                last.then_inc(y_ready[u], 1)

            one_ahead(pe, front, back, NB // 2)

        @block.scalar
        def _(act):
            def front(i, u):
                act.wait_ge(turned[u], i + 1)
                wait(act, y_ready[u], i)
                act.copy(cT[:, u, :], p_cT[:, u, :]).then_inc(cT_ready[u], 1)

            def back(i, u):
                act.wait_ge(added[u], i + 1)
                act.copy(x_by_seq[:, 2 * i + u], y[:, u]).then_inc(kept[u], 1)

            one_ahead(act, front, back, NB // 2)

        @block.vector
        def _(dve):
            def front(i, u):
                wait(dve, turned[u], i)
                dve.tensor_copy(cx[:, u], ctx_by_seq[:, 2 * i + u]).then_inc(copied[u], 1)

            def back(i, u):
                b = 2 * i + u
                dve.wait_ge(y_ready[u], i + 1)
                wait(dve, kept[u], i)
                dve.tensor_tensor(y[:, u], p_y[:, u],
                                  w["bo"][:].rearrange("p (o d) -> p o d", o=1).to_broadcast([P, TPB, D]),
                                  ALU.add).then_inc(biased[u], 1)
                dve.wait_ge(biased[u], i + 1)
                dve.tensor_tensor(y[:, u], x_by_seq[:, b], y[:, u], ALU.add).then_inc(added[u], 1)
                dve.wait_ge(added[u], i + 1)
                wait(dve, counted[u], 2 * i)
                for t in range(TPB):
                    last = dve.bn_stats(st[:, u, t, :], y[:, u, t, :])
                last.then_inc(counted[u], 1)
                dve.wait_ge(counted[u], 2 * i + 1)
                dve.tensor_copy(stats[:].rearrange("p (b t) s -> p b t s", t=TPB)[:, b], st[:, u])\
                   .then_inc(counted[u], 1)

            one_ahead(dve, front, back, NB // 2)


def route(nc, name, x, mean, rstd, w, identity, positions, weights, slot_group):
    NS = RG + EXPERTS
    with Phase(nc, name) as ph:
        xn = ph.sb("xn", [P, 2, TPB, D], F32)
        xT = ph.sb("xT", [P, 2, SEQ], F32)
        logits = ph.sb("logits", [P, NT, NS], F32)
        sig = ph.sb("sig", [P, NT, NS], F32)
        top = ph.sb("top", [P, NT], F32)
        top_w = ph.sb("top_w", [P, 2, NT], F32)
        taken = ph.sb("taken", [P, NT], F32)
        equal = ph.sb("equal", [P, NT, RG], F32)
        onehot = ph.sb("onehot", [P, NT, RG], F32)
        onehot_bf = ph.sb("onehot_bf", [P, NT, RG], BF16)
        chosen = ph.sb("chosen", [P, NT, RG, EPG], F32)
        micro = ph.sb("micro", [P, NT, EPG], F32)
        micro_sum = ph.sb("micro_sum", [P, NT], F32)
        counts = ph.sb("counts", [P, 3, NT, RG], F32)
        padded = ph.sb("padded", [P, RG], I32)
        starts = ph.sb("starts", [P, 2, RG], F32)
        place = ph.sb("place", [P, NT, RG], F32)
        place_sum = ph.sb("place_sum", [P, NT], F32)
        slot_f = ph.sb("slot_f", [P, 2, SLOTS], F32)
        p_xT = ph.ps("p_xT", [P, 2, SEQ])
        p_log = ph.ps("p_log", [P, 2, SEQ])
        p_rank = ph.ps("p_rank", [P, 2, SEQ])
        xn_ready, turned, xT_ready, log_ready, log_copied = (
            ph.sems(n, 2) for n in ("xn_ready", "turned", "xT_ready", "log_ready", "log_copied"))
        sig_ready, onehot_ready, rank_ready, dve_step = (
            ph.sem(n) for n in ("sig_ready", "onehot_ready", "rank_ready", "dve_step"))
        block = ph.block()

        @block.tensor
        def _(pe):
            def front(i, u):
                pe.wait_ge(xn_ready[u], i + 1)
                wait(pe, xT_ready[u], i)
                for t in range(TPB):
                    last = pe.transpose(p_xT[:, u, t * P:(t + 1) * P], xn[:, u, t, :], identity[:])
                last.then_inc(turned[u], 1)

            def back(i, u):
                pe.wait_ge(xT_ready[u], i + 1)
                wait(pe, log_copied[u], i)
                for t in range(TPB):
                    last = pe.matmul(p_log[:, u, NS * t:NS * (t + 1)], xT[:, u, t * P:(t + 1) * P],
                                     w["router"][:], start=True, stop=True)
                last.then_inc(log_ready[u], 1)

            one_ahead(pe, front, back, NB // 2)
            pe.wait_ge(onehot_ready, 1)
            flat = onehot_bf[:].rearrange("p t g -> p (t g)")
            pe.matmul(p_rank[:, 0, 0:NT * RG], w["before"][:], flat, start=True, stop=True)
            pe.matmul(p_rank[:, 1, 0:NT * RG], w["ones"][:], flat, start=True, stop=True).then_inc(rank_ready, 1)

        @block.scalar
        def _(act):
            def step(i, u):
                act.wait_ge(turned[u], i + 1)
                wait(act, log_ready[u], i)
                act.copy(xT[:, u, :], p_xT[:, u, :]).then_inc(xT_ready[u], 1)

            in_turns(act, step, NB // 2, 2)
            for u in range(2):
                act.wait_ge(log_copied[u], NB // 2)
            act.activation(sig[:], logits[:], ACT.Sigmoid).then_inc(sig_ready, 1)

        @block.vector
        def _(dve):
            def front(i, u):
                b = 2 * i + u
                wait(dve, turned[u], i)
                for t in range(TPB):
                    tile = TPB * b + t
                    last = dve.tensor_scalar(xn[:, u, t, :], x[:, tile, :], mean[:, bass.ds(tile, 1)],
                                             rstd[:, bass.ds(tile, 1)], ALU.subtract, ALU.mult)
                last.then_inc(xn_ready[u], 1)

            def back(i, u):
                b = 2 * i + u
                dve.wait_ge(log_ready[u], i + 1)
                dve.tensor_copy(logits[:].rearrange("p (b t) n -> p b (t n)", t=TPB)[:, b],
                                p_log[:, u, 0:TPB * NS]).then_inc(log_copied[u], 1)

            one_ahead(dve, front, back, NB // 2)
            dve.wait_ge(sig_ready, 1)
            done = [0]

            def then(instruction):
                done[0] += 1
                instruction.then_inc(dve_step, 1)
                dve.wait_ge(dve_step, done[0])

            then(dve.tensor_reduce(top[:], sig[:, :, 0:RG], AX.X, ALU.max))
            then(dve.tensor_tensor(equal[:], sig[:, :, 0:RG],
                                   top[:].rearrange("p (t o) -> p t o", o=1).to_broadcast([P, NT, RG]), ALU.is_equal))
            dve.tensor_copy(onehot[:, :, 0], equal[:, :, 0])
            then(dve.tensor_copy(taken[:], equal[:, :, 0]))
            for g in range(1, RG):
                dve.tensor_tensor(onehot[:, :, g], equal[:, :, g], taken[:], ALU.is_gt)
                then(dve.tensor_tensor(taken[:], equal[:, :, g], taken[:], ALU.max))
            dve.tensor_copy(onehot_bf[:], onehot[:]).then_inc(onehot_ready, 1)
            then(dve.tensor_scalar(top_w[:, 0], top[:], EPS_TOPK, None, ALU.add))
            then(dve.reciprocal(top_w[:, 1], top_w[:, 0]))
            then(dve.tensor_tensor(top_w[:, 0], top[:], top_w[:, 1], ALU.mult))
            then(dve.tensor_tensor(chosen[:], sig[:, :, RG:NS].rearrange("p t (g e) -> p t g e", g=RG),
                                   onehot[:].rearrange("p t (g o) -> p t g o", o=1).to_broadcast([P, NT, RG, EPG]),
                                   ALU.mult))
            then(dve.tensor_reduce(micro[:], chosen[:].rearrange("p t g e -> p t e g"), AX.X, ALU.add))
            then(dve.tensor_tensor(micro_sum[:], micro[:, :, 0], micro[:, :, 1], ALU.add))
            then(dve.tensor_scalar(micro_sum[:], micro_sum[:], EPS_TOPK, None, ALU.add))
            then(dve.reciprocal(top_w[:, 1], micro_sum[:]))
            for e in range(EPG):
                then(dve.tensor_tensor(micro[:, :, e], micro[:, :, e], top_w[:, 1], ALU.mult))
                then(dve.tensor_tensor(weights[:, :, e], micro[:, :, e], top_w[:, 0], ALU.mult))
            dve.wait_ge(rank_ready, 1)
            totals = p_rank[:, 1, 0:NT * RG].rearrange("p (t g) -> p t g", g=RG)
            then(dve.tensor_copy(counts[:, 0], totals))
            cur, shift = 0, 1
            while shift < NT:
                dve.tensor_copy(counts[:, 1 - cur, 0:shift], counts[:, cur, 0:shift])
                then(dve.tensor_tensor(counts[:, 1 - cur, shift:NT], counts[:, cur, shift:NT],
                                       counts[:, cur, 0:NT - shift], ALU.add))
                cur, shift = 1 - cur, 2 * shift
            running = counts[:, cur]
            then(dve.tensor_scalar(padded[:], running[:, NT - 1, :], float(P - 1), None, ALU.add))
            then(dve.tensor_scalar(padded[:], padded[:], 7, 7, ALU.logical_shift_right, ALU.logical_shift_left))
            then(dve.tensor_copy(starts[:, 0], padded[:]))
            then(dve.memset(starts[:, 1, 0:1], 0.0))
            for g in range(1, RG):
                then(dve.tensor_tensor(starts[:, 1, g:g + 1], starts[:, 1, g - 1:g], starts[:, 0, g - 1:g], ALU.add))
            then(dve.tensor_tensor(place[:], running, totals, ALU.subtract))
            then(dve.tensor_tensor(place[:], place[:], p_rank[:, 0, 0:NT * RG].rearrange("p (t g) -> p t g", g=RG),
                                   ALU.add))
            then(dve.tensor_tensor(place[:], place[:],
                                   starts[:, 1].rearrange("p (o g) -> p o g", o=1).to_broadcast([P, NT, RG]), ALU.add))
            then(dve.tensor_tensor(place[:], place[:], onehot[:], ALU.mult))
            then(dve.tensor_reduce(place_sum[:], place[:], AX.X, ALU.add))
            then(dve.tensor_copy(positions[:], place_sum[:]))
            then(dve.tensor_scalar(slot_f[:, 0], w["slot_rows"][:], starts[:, 1, 1:2], None, ALU.is_ge))
            for g in range(2, RG):
                then(dve.tensor_scalar(slot_f[:, 1], w["slot_rows"][:], starts[:, 1, g:g + 1], None, ALU.is_ge))
                then(dve.tensor_tensor(slot_f[:, 0], slot_f[:, 0], slot_f[:, 1], ALU.add))
            then(dve.tensor_copy(slot_group[:], slot_f[0:1, 0]))


def scatter_rows(nc, name, x, mean, rstd, positions, weights, sorted_rows, clear):
    with Phase(nc, name) as ph:
        NR = 4
        zero = ph.sb("zero", [P, SLOTS * ROW // 4], F32)
        rows = [ph.sb(f"rows{u}", [P, ROW], F32) for u in range(NR)]
        index = [ph.sb(f"index{u}", [P, 1], U32) for u in range(NR)]
        zeroed, cleared, begun = ph.sem("zeroed"), ph.sem("cleared"), ph.sem("begun")
        ready, written = ph.sems("ready", NR), ph.software_sems(NR)
        block = ph.block()

        if clear:
            @block.sync
            def _(sp):
                sp.wait_ge(zeroed, 1)
                flat = sorted_rows.rearrange("(q p s) c -> q p (s c)", q=4, p=P)
                for q in range(4):
                    sp.dma_start(flat[q], zero[:]).then_inc(cleared, 16)

        @block.vector
        def _(dve):
            if clear:
                dve.memset(zero[:], 0.0).then_inc(zeroed, 1)
            def step(i, u):
                t = NR * i + u
                wait(dve, written[u], 16 * i)
                dve.tensor_scalar(rows[u][:, 0:D], x[:, t, :], mean[:, bass.ds(t, 1)], rstd[:, bass.ds(t, 1)],
                                  ALU.subtract, ALU.mult)
                dve.tensor_copy(rows[u][:, D:ROW], weights[:, t, :])
                dve.tensor_copy(index[u][:], positions[:, bass.ds(t, 1)]).then_inc(ready[u], 1)

            in_turns(dve, step, NT // NR, NR)

        @block.gpsimd
        def _(pool):
            if clear:
                pool.wait_ge(cleared, 16 * 4)
            def step(i, u):
                pool.wait_ge(ready[u], i + 1)
                pool.sem_inc(begun, 1)
                pool.indirect_dma_start(sorted_rows, bass.IndirectOffsetOnAxis(ap=index[u][:, 0:1], axis=0),
                                        rows[u][:], None).then_inc(written[u], 16)

            in_turns(pool, step, NT // NR, NR)
            for u in range(NR):
                pool.wait_ge(written[u], 16 * (NT // NR))


def experts(nc, name, sorted_rows, sorted_out, slot_group, w, identity):
    with Phase(nc, name) as ph:
        rows = ph.sb("rows", [P, 2, ROW], F32)
        xT = ph.sb("xT", [P, 2, P], F32)
        act_g = ph.sb("act_g", [P, 2, EPG, FF], F32)
        hidden = ph.sb("hidden", [P, 2, EPG, FF], F32)
        hT = ph.sb("hT", [P, 2, DNC * P], F32)
        y = ph.sb("y", [P, 2, D], F32)
        p_gu = ph.ps("p_gu", [P, 2, EPG, 2 * FF])
        p_hT = ph.ps("p_hT", [P, 1, SEQ])
        p_xT = ph.ps("p_xT", [P, 2, SEQ])
        p_y = ph.ps("p_y", [P, SEQ])
        loaded, stored = ph.sems("loaded", 2), ph.software_sems(2)
        x_turned, xT_ready, gu_ready, silu_ready = (ph.sem(n) for n in ("x_turned", "xT_ready", "gu_ready", "silu_ready"))
        hidden_ready, h_turned, hT_ready, y_ready, y_copied = (
            ph.sem(n) for n in ("hidden_ready", "h_turned", "hT_ready", "y_ready", "y_copied"))
        block = ph.block()

        def pipeline(eng, step):
            for s in range(4):
                step(s // 2, s % 2)
            with eng.Fori(2, SLOTS // 2 - 1) as i:
                for u in range(2):
                    step(i, u)
            for s in range(SLOTS - 2, SLOTS + 1):
                step(s // 2, s % 2)

        def first(s):
            return isinstance(s, int) and s == 0

        def last_slot(s):
            return isinstance(s, int) and s == SLOTS - 1

        def past(s):
            return isinstance(s, int) and s == SLOTS

        @block.sync
        def _(sp):
            def step(i, u):
                s = 2 * i + u
                if past(s):
                    return
                wait(sp, hidden_ready, s - 1)
                wait(sp, x_turned, s - 1)
                sp.dma_start(rows[:, u, :], sorted_rows.rearrange("(s p) c -> s p c", p=P)[s]).then_inc(loaded[u], 16)

            pipeline(sp, step)

        @block.scalar
        def _(act):
            def step(i, u):
                s = 2 * i + u
                if not first(s):
                    act.wait_ge(h_turned, s)
                    wait(act, y_ready, s - 2)
                    act.copy(hT[:, 1 - u, :], p_hT[:, 0, :]).then_inc(hT_ready, 1)
                if not past(s):
                    act.wait_ge(gu_ready, s + 1)
                    wait(act, hidden_ready, s - 1)
                    act.activation(act_g[:, u], p_gu[:, u, :, 0:FF], ACT.Silu).then_inc(silu_ready, 1)

            pipeline(act, step)

        @block.vector
        def _(dve):
            def copy_xT(i, u, s):
                dve.wait_ge(x_turned, s + 1)
                wait(dve, gu_ready, s - 1)
                dve.tensor_copy(xT[:, u, :], p_xT[:, u, 0:P]).then_inc(xT_ready, 1)

            def step(i, u):
                s = 2 * i + u
                if first(s):
                    copy_xT(0, 0, 0)
                if not (past(s) or last_slot(s)):
                    copy_xT(i, 1 - u, s + 1)
                if not past(s):
                    dve.wait_ge(silu_ready, s + 1)
                    wait(dve, h_turned, s - 1)
                    for e in range(EPG):
                        last = dve.scalar_tensor_tensor(hidden[:, u, e, :], act_g[:, u, e, :], rows[:, u, D + e:D + e + 1],
                                                        p_gu[:, u, e, FF:2 * FF], ALU.mult, ALU.mult)
                    last.then_inc(hidden_ready, 1)
                if not first(s):
                    dve.wait_ge(y_ready, s)
                    wait(dve, stored[1 - u], 16 * ((i - 1) if u == 0 else i))
                    dve.tensor_copy(y[:, 1 - u, :], p_y[:, 0:D]).then_inc(y_copied, 1)

            pipeline(dve, step)

        @block.gpsimd
        def _(pool):
            def step(i, u):
                s = 2 * i + u
                if not (isinstance(s, int) and s == 0):
                    pool.wait_ge(y_copied, s)
                    pool.dma_start(sorted_out.rearrange("(s p) c -> s p c", p=P)[s - 1], y[:, 1 - u, :])\
                        .then_inc(stored[1 - u], 16)

            pipeline(pool, step)
            for u in range(2):
                pool.wait_ge(stored[u], 16 * (SLOTS // 2))

        @block.tensor
        def _(pe):
            gu = w["gate_up"][:].rearrange("p (g e) f -> p g e f", g=RG)
            dn = w["down"][:].rearrange("p (g c) d -> p g c d", g=RG)

            def group_of(s):
                return pe.value_load(slot_group[0:1, bass.ds(s, 1)], min_val=0, max_val=RG - 1)

            def turn_x(i, u, s):
                pe.wait_ge(loaded[u], 16 * (i + 1))
                wait(pe, xT_ready, s - 1)
                pe.transpose(p_xT[:, u, 0:P], rows[:, u, 0:D], identity[:]).then_inc(x_turned, 1)

            def gate_up(group, u, e):
                last = pe.matmul(p_gu[:, u, e, :], xT[:, u, :], gu[:, group, e, :], start=True, stop=True)
                if e == EPG - 1:
                    last.then_inc(gu_ready, 1)

            def step(i, u):
                s = 2 * i + u
                group = None if past(s) else group_of(s)
                group_before = None if first(s) else group_of(s - 1)
                if first(s):
                    turn_x(0, 0, 0)
                if not past(s):
                    pe.wait_ge(xT_ready, s + 1)
                    wait(pe, hidden_ready, s - 1)
                    gate_up(group, u, 0)
                if not first(s):
                    pe.wait_ge(hidden_ready, s)
                    wait(pe, hT_ready, s - 1)
                    for c in range(DNC):
                        last = pe.transpose(p_hT[:, 0, c * P:(c + 1) * P],
                                            hidden[:, 1 - u].rearrange("p e f -> p (e f)")[:, c * P:(c + 1) * P],
                                            identity[:])
                    last.then_inc(h_turned, 1)
                if not (past(s) or last_slot(s)):
                    turn_x(i + u, 1 - u, s + 1)
                if not past(s):
                    gate_up(group, u, 1)
                if not first(s):
                    pe.wait_ge(hT_ready, s)
                    wait(pe, y_copied, s - 1)
                    for c in range(DNC):
                        last = pe.matmul(p_y[:, 0:D], hT[:, 1 - u, c * P:(c + 1) * P], dn[:, group_before, c, :],
                                         start=(c == 0), stop=(c == DNC - 1))
                    last.then_inc(y_ready, 1)

            pipeline(pe, step)


def gather_rows(nc, name, x, positions, sorted_out, stats):
    with Phase(nc, name) as ph:
        NR = 4
        rows = [ph.sb(f"rows{u}", [P, D], F32) for u in range(NR)]
        index = [ph.sb(f"index{u}", [P, 1], U32) for u in range(NR)]
        st = ph.sb("st", [P, NR, 6], F32)
        indexed, fetched, added = ph.sems("indexed", NR), ph.software_sems(NR), ph.sems("added", NR)
        counted, kept = ph.sems("counted", NR), ph.sems("kept", NR)
        begun = ph.sem("begun")
        block = ph.block()

        @block.scalar
        def _(act):
            def name_rows(i, u):
                wait(act, fetched[u], 16 * i)
                act.copy(index[u][:], positions[:, bass.ds(NR * i + u, 1)]).then_inc(indexed[u], 1)

            def keep(i, u):
                act.wait_ge(added[u], i + 1)
                act.copy(x[:, NR * i + u, :], rows[u][:])
                act.wait_ge(counted[u], i + 1)
                act.copy(stats[:, NR * i + u, :], st[:, u, :]).then_inc(kept[u], 1)

            for u in range(NR):
                name_rows(0, u)
            with act.Fori(1, NT // NR) as i:
                for u in range(NR):
                    name_rows(i, u)
                    keep(i - 1, u)
            for u in range(NR):
                keep(NT // NR - 1, u)

        @block.gpsimd
        def _(pool):
            def step(i, u):
                pool.wait_ge(indexed[u], i + 1)
                wait(pool, kept[u], i)
                pool.sem_inc(begun, 1)
                pool.indirect_dma_start(rows[u][:], None, sorted_out,
                                        bass.IndirectOffsetOnAxis(ap=index[u][:, 0:1], axis=0))\
                    .then_inc(fetched[u], 16)

            in_turns(pool, step, NT // NR, NR)

        @block.vector
        def _(dve):
            def step(i, u):
                dve.wait_ge(fetched[u], 16 * (i + 1))
                dve.tensor_tensor(rows[u][:], x[:, NR * i + u, :], rows[u][:], ALU.add).then_inc(added[u], 1)
                dve.wait_ge(added[u], i + 1)
                dve.bn_stats(st[:, u, :], rows[u][:]).then_inc(counted[u], 1)

            in_turns(dve, step, NT // NR, NR)


def build(nc, a, out):
    with Phase(nc, "all") as ph:
        Phase.own_sems = [ph.sem(f"software_dma{i}") for i in range(2 * (4 + 2 + 4))]
        x = ph.sb("x", [P, NT, D], F32)
        stats = ph.sb("stats", [P, NT, 6], F32)
        mean, rstd = ph.sb("mean", [P, NT], F32), ph.sb("rstd", [P, NT], F32)
        before = ph.sb("before_f", [P, P], F32)
        identity, identity_bf = ph.sb("identity", [P, P], F32), ph.sb("identity_bf", [P, P], BF16)
        positions = ph.sb("positions", [P, NT], U32)
        weights = ph.sb("weights", [P, NT, EPG], F32)
        slot_group = ph.sb("slot_group", [1, SLOTS], I32)
        ffn = {"gate_up": ph.sb("gate_up", [P, EXPERTS, 2 * FF], F32), "down": ph.sb("down", [P, EXPERTS * 2, D], F32),
               "router": ph.sb("router", [P, RG + EXPERTS], F32), "before": ph.sb("before", [P, P], BF16),
               "ones": ph.sb("ones", [P, P], BF16), "slot_rows": ph.sb("slot_rows", [P, SLOTS], F32)}
        wa, wb = ({k: ph.sb(f"{n}_{k}", [P, P], F32) for k in ("q", "k", "v", "o", "bv", "bo")} |
                  {k: ph.sb(f"{n}_{k}", [P, 1], F32) for k in ("bq", "bk", "gamma", "beta")} for n in "ab")
        q_parts = nc.dram_tensor("q_parts", [3, NG, HG * HD, SEQ], BF16, kind="Internal").ap()
        k_parts = nc.dram_tensor("k_parts", [3, NG, HG * HD, SEQ], BF16, kind="Internal").ap()
        v_strips = nc.dram_tensor("v_strips", [NG, P, TPB, HG * VW], F32, kind="Internal").ap()
        sorted_rows = nc.dram_tensor("sorted_rows", [SLOTS * P, ROW], F32, kind="Internal").ap()
        sorted_out = nc.dram_tensor("sorted_out", [SLOTS * P, D], F32, kind="Internal").ap()
        scratch = (q_parts, k_parts, v_strips)

        def column(v):
            return v.rearrange("(d o) -> d o", o=1)

        def on_all_rows(v):
            return v.rearrange("(o d) -> o d", o=1).to_broadcast([P, v.shape[0]])

        x_in = a["L0_attn_a_x"].rearrange("b (t p) d -> p (b t) d", p=P)
        loads = [(x[:, NT // 4 * q:NT // 4 * (q + 1), :], x_in[:, NT // 4 * q:NT // 4 * (q + 1), :]) for q in range(4)]
        loads += [(wa[k][:], a["L0_attn_a_W_qkv"][:, i * D:(i + 1) * D]) for i, k in enumerate("qkv")]
        bias = a["L0_attn_a_b_qkv"]
        loads += [(wa["o"][:], a["L0_attn_a_W_proj"]), (wa["bo"][:], on_all_rows(a["L0_attn_a_b_proj"])),
                  (wa["bq"][:], column(bias[0:D])), (wa["bk"][:], column(bias[D:2 * D])),
                  (wa["bv"][:], on_all_rows(bias[2 * D:3 * D])),
                  (wa["gamma"][:], column(a["L0_attn_a_ln_gamma"])), (wa["beta"][:], column(a["L0_attn_a_ln_beta"]))]
        loads += [(wb[k][:], a[n]) for k, n in (("q", "WqT"), ("k", "WkT"), ("v", "WvT"), ("o", "WoT"))]
        loads += [(ffn["gate_up"][:, :, 0:FF], a["L0_ffn_gate_w"].rearrange("n d f -> d n f")),
                  (ffn["gate_up"][:, :, FF:2 * FF], a["L0_ffn_up_w"].rearrange("n d f -> d n f")),
                  (ffn["down"][:], a["L0_ffn_down_w"].rearrange("n (h p) d -> p (n h) d", p=P)),
                  (ffn["router"][:, 0:RG], a["L0_ffn_macro_w"]),
                  (ffn["router"][:, RG:].rearrange("p (g e) -> p g e", g=RG),
                   a["L0_ffn_micro_w"].rearrange("g d e -> d g e")),
                  (identity[:], a["identity"]), (before[:], a["before"]),
                  (ffn["slot_rows"][:], a["slot_rows"])]
        with Phase(nc, "load") as ld:
            x_landed, weights_landed = ld.sems("x_landed", 4), ld.sem("weights_landed")
            block = ld.block()

            @block.sync
            def _(sp):
                for q, (dst, src) in enumerate(loads[0:4]):
                    sp.dma_start(dst, src).then_inc(x_landed[q], 16)
                for dst, src in loads[4:]:
                    sp.dma_start(dst, src).then_inc(weights_landed, 16)
                sp.wait_ge(weights_landed, 16 * len(loads[4:]))

            @block.vector
            def _(dve):
                for q in range(4):
                    dve.wait_ge(x_landed[q], 16)
                    for t in range(NT // 4 * q, NT // 4 * (q + 1)):
                        dve.bn_stats(stats[:, t, :], x[:, t, :])

        with Phase(nc, "const") as c:
            block = c.block()

            @block.vector
            def _(dve):
                dve.tensor_copy(identity_bf[:], identity[:])
                dve.tensor_copy(ffn["before"][:], before[:])
                dve.memset(ffn["ones"][:], 1.0)
                for k in ("bv", "bo", "bq", "bk", "beta"):
                    dve.memset(wb[k][:], 0.0)
                dve.memset(wb["gamma"][:], 1.0)

        def mixture(n, clear):
            finish_stats(nc, f"{n}s", stats, mean, rstd, False)
            route(nc, f"{n}r", x, mean, rstd, ffn, identity, positions, weights, slot_group)
            scatter_rows(nc, f"{n}c", x, mean, rstd, positions, weights, sorted_rows, clear)
            experts(nc, f"{n}e", sorted_rows, sorted_out, slot_group, ffn, identity)
            gather_rows(nc, f"{n}g", x, positions, sorted_out, stats)

        def attention(n, w, twice, masks):
            with Phase(nc, n) as p2:
                ctx = p2.sb("ctx", [P, NT, D], F32)
                finish_stats(nc, f"{n}s", stats, mean, rstd, twice)
                project(nc, f"{n}p", x, mean, rstd, w, scratch, identity)
                attend(nc, f"{n}a", scratch, ctx, identity, identity_bf, masks)
                attention_out(nc, f"{n}o", x, ctx, w, identity, stats)

        attention("A", wa, True, None)
        mixture("F", True)
        with Phase(nc, "m") as mk:
            masks = mk.sb("masks", [P, 2, 2, TPB, SEQ], BF16)
            with Phase(nc, "mf") as mf:
                masks_f = mf.sb("masks_f", [P, 2, 2, TPB, SEQ], F32)
                landed = mf.sems("landed", 2)
                block = mf.block()

                @block.sync
                def _(sp):
                    for kind in range(2):
                        sp.dma_start(masks_f[:, kind], a["masks"][:, kind]).then_inc(landed[kind], 16)

                @block.vector
                def _(dve):
                    for kind in range(2):
                        dve.wait_ge(landed[kind], 16)
                        dve.tensor_copy(masks[:, kind], masks_f[:, kind])
            attention("B", wb, False, masks)
        mixture("G", False)
        with Phase(nc, "out") as o:
            stored = o.sem("stored")
            block = o.block()

            @block.sync
            def _(sp):
                out_v = out.rearrange("b (t p) d -> p (b t) d", p=P)
                for q in range(4):
                    sp.dma_start(out_v[:, NT // 4 * q:NT // 4 * (q + 1), :], x[:, NT // 4 * q:NT // 4 * (q + 1), :]).then_inc(stored, 16)
                sp.wait_ge(stored, 16 * 4)


def shape_constants():
    import numpy as np

    stride = int(np.sqrt(SEQ))
    i, j = np.arange(SEQ)[:, None], np.arange(SEQ)[None, :]
    causal = j <= i
    seen = [causal & ((i - j < stride) | (j % stride == i % stride)),
            causal & ((j // stride == i // stride) | (j % stride >= stride - 1))]
    masks = np.zeros((P, 2, 2, TPB, SEQ), np.float32)
    for kind, ok in enumerate(seen):
        bias = np.where(ok, 0.0, -3e38).astype(np.float32)
        for t in range(TPB):
            masks[:, kind, 0, t, :] = bias[t * P:(t + 1) * P, :]
            masks[:, kind, 1, t, :] = bias[:, t * P:(t + 1) * P].T
    return {"identity": np.eye(P, dtype=np.float32), "before": np.triu(np.ones((P, P), np.float32), 1),
            "slot_rows": np.tile(np.arange(SLOTS, dtype=np.float32) * P, (P, 1)),
            "masks": masks}


def kernel(**inputs):
    import numpy as _np
    import concourse.bacc as _bacc
    from concourse import mybir as _mybir
    from concourse.bass_utils import run_bass_kernel_spmd as _run

    nc = _bacc.Bacc("TRN2", target_bir_lowering=False, num_devices=1)
    given = {}
    for name, value in inputs.items():
        if name in ("L0_attn_b_Wq", "L0_attn_b_Wk", "L0_attn_b_Wv", "L0_attn_b_Wo"):
            given[name[-2:] + "T"] = _np.ascontiguousarray(_np.asarray(value).T)
        else:
            given[name] = _np.ascontiguousarray(value)
    given.update(shape_constants())
    arrays, args = {}, {}
    for name, v in given.items():
        arrays[f"in_{name}"] = v
        args[name] = nc.dram_tensor(f"in_{name}", v.shape, _mybir.dt.from_np(v.dtype), kind="ExternalInput").ap()
    out = nc.dram_tensor("out_0", [NB, SEQ, D], _mybir.dt.float32, kind="ExternalOutput").ap()
    build(nc, args, out)
    r = _run(nc, [arrays], core_ids=[0])
    return r.results[0]["out_0"]
```

```python
from contextlib import ExitStack

import concourse.bass as bass
from concourse import mybir

P = 128
NB, SEQ, D = 16, 512, 128
HEADS, HD = 16, 8
TPB = SEQ // P
NT = NB * TPB
HG = 4
NG = NB * HEADS // HG
VW = P // HG
EXPERTS, FF, RG = 8, 256, 4
EPG = EXPERTS // RG
GUW = EPG * 2 * FF
DNC = EPG * FF // P
SLOTS = NT + RG
ROW = D + EPG
SCALE = HD ** -0.5
EPS_LN, EPS_TOPK, EPS_DEN = 1e-5, 1e-9, 1e-12
REPEATS = [3, 2, 1]
MROW = 64
STRIDE = int(SEQ ** 0.5)
SPECIAL = [(STRIDE - 1, SEQ, STRIDE)] + [(t * P // STRIDE * STRIDE, t * P, 1)
                                         for t in range(1, TPB) if t * P % STRIDE]
SPECIAL_KEYS = [key for piece in SPECIAL for key in range(*piece)]
NSP = len(SPECIAL_KEYS)
KEYS = SEQ + P

F32, BF16, I32, U32 = mybir.dt.float32, mybir.dt.bfloat16, mybir.dt.int32, mybir.dt.uint32
ALU = mybir.AluOpType
ACT = mybir.ActivationFunctionType
AX = mybir.AxisListType


def wait(eng, sem, value):
    if not isinstance(value, int) or value > 0:
        eng.wait_ge(sem, value)


def in_turns(eng, step, rounds, buffers):
    for u in range(buffers):
        step(0, u)
    with eng.Fori(1, rounds) as i:
        for u in range(buffers):
            step(i, u)


def one_ahead(eng, front, back, rounds):
    front(0, 0)
    front(0, 1)
    back(0, 0)
    front(1, 0)
    back(0, 1)
    with eng.Fori(1, rounds - 1) as i:
        for u in range(2):
            front(i + u, 1 - u)
            back(i, u)
    front(rounds - 1, 1)
    back(rounds - 1, 0)
    back(rounds - 1, 1)


def two_ahead(eng, front, back, rounds):
    front(0, 0)
    front(0, 1)
    for u in range(2):
        front(1, u)
        back(0, u)
    with eng.Fori(1, rounds - 1) as i:
        for u in range(2):
            front(i + 1, u)
            back(i, u)
    back(rounds - 1, 0)
    back(rounds - 1, 1)


class Phase:

    own_sems = []

    def __init__(self, nc, name):
        self.nc, self.name, self.ctx = nc, name, ExitStack()
        self.used, self.blocks = [], []

    def __enter__(self):
        self.ctx.__enter__()
        return self

    def __exit__(self, *a):
        if self.blocks:
            self.blocks.pop().__exit__(*a)
            if self.used and a[0] is None:
                with self.nc.Block() as clear:
                    @clear.sync
                    def _(sp):
                        for sem in self.used:
                            sp.sem_clear(sem)
        return self.ctx.__exit__(*a)

    def sb(self, name, shape, dt):
        return self.ctx.enter_context(self.nc.sbuf_tensor(f"{self.name}_{name}", shape, dt))

    def ps(self, name, shape, dt=F32):
        return self.ctx.enter_context(self.nc.psum_tensor(f"{self.name}_{name}", shape, dt))

    def sem(self, name):
        self.used.append(self.ctx.enter_context(self.nc.semaphore(f"{self.name}_{name}")))
        return self.used[-1]

    def software_sems(self, n):
        return [self.own_sems.pop() for _ in range(n)]

    def sems(self, name, n):
        return [self.sem(f"{name}{i}") for i in range(n)]

    def block(self):
        self.blocks.append(self.nc.Block())
        return self.blocks[-1].__enter__()


def load_constants(nc, name, loads):
    with Phase(nc, name) as ph:
        landed = ph.sem("landed")
        block = ph.block()

        @block.sync
        def _(sp):
            for dst, src in loads:
                sp.dma_start(dst, src).then_inc(landed, 16)
            sp.wait_ge(landed, 16 * len(loads))


def finish_stats(nc, name, stats, mean, rstd, twice):
    with Phase(nc, name) as ph:
        tmp = ph.sb("tmp", [P, NT], F32)
        var = ph.sb("var", [P, NT], F32)
        inner = ph.sb("inner", [P, 2, NT], F32)
        dve_step, var_ready, std_ready = ph.sem("dve_step"), ph.sem("var_ready"), ph.sem("std_ready")
        block = ph.block()

        @block.vector
        def _(dve):
            dve.tensor_tensor(tmp[:], stats[:, :, 1], stats[:, :, 4], ALU.subtract)
            dve.tensor_tensor(var[:], stats[:, :, 2], stats[:, :, 5], ALU.add)
            dve.tensor_tensor(mean[:], stats[:, :, 1], stats[:, :, 4], ALU.add).then_inc(dve_step, 1)
            dve.wait_ge(dve_step, 1)
            dve.tensor_tensor(tmp[:], tmp[:], tmp[:], ALU.mult)
            dve.tensor_scalar(var[:], var[:], 1.0 / D, None, ALU.mult)
            dve.tensor_scalar(mean[:], mean[:], 0.5, None, ALU.mult).then_inc(dve_step, 1)
            dve.wait_ge(dve_step, 2)
            dve.scalar_tensor_tensor(inner[:, 0], tmp[:], 0.25, var[:], ALU.mult, ALU.add).then_inc(dve_step, 1)
            dve.wait_ge(dve_step, 3)
            dve.tensor_scalar(var[:], inner[:, 0], EPS_LN, None, ALU.add).then_inc(var_ready, 1)
            dve.wait_ge(std_ready, 1)
            dve.reciprocal(rstd[:], tmp[:]).then_inc(dve_step, 1)
            if twice:
                dve.wait_ge(dve_step, 4)
                dve.tensor_tensor(inner[:, 1], rstd[:], rstd[:], ALU.mult).then_inc(dve_step, 1)
                dve.wait_ge(dve_step, 5)
                dve.tensor_tensor(inner[:, 0], inner[:, 0], inner[:, 1], ALU.mult).then_inc(dve_step, 1)
                dve.wait_ge(dve_step, 6)
                dve.tensor_scalar(var[:], inner[:, 0], EPS_LN, None, ALU.add).then_inc(var_ready, 1)
                dve.wait_ge(std_ready, 2)
                dve.reciprocal(inner[:, 1], tmp[:]).then_inc(dve_step, 1)
                dve.wait_ge(dve_step, 7)
                dve.tensor_tensor(rstd[:], rstd[:], inner[:, 1], ALU.mult)

        @block.scalar
        def _(act):
            for n in range(2 if twice else 1):
                act.wait_ge(var_ready, n + 1)
                act.activation(tmp[:], var[:], ACT.Sqrt).then_inc(std_ready, 1)


def project(nc, name, src, mean, rstd, w, scratch, identity, special):
    q_parts, k_parts, v_strips = scratch
    with Phase(nc, name) as ph:
        xn = ph.sb("xn", [P, 2, TPB, D], F32)
        xT = ph.sb("xT", [P, 2, SEQ], F32)
        parts = ph.sb("parts", [P, 2, 2, 3, KEYS], BF16)
        x_special = ph.sb("x_special", [P, 2, P], F32)
        rest = ph.sb("rest", [P, 2, 2, SEQ], F32)
        VT = TPB + 1 if special else TPB
        KW = KEYS if special else SEQ
        strips = ph.sb("strips", [P, 2, HEADS // HG, VT, HG, VW], F32)
        scaled = ph.sb("scaled", [P, P + 1], F32)
        p_xT = ph.ps("p_xT", [P, 2, SEQ])
        p_qk = ph.ps("p_qk", [P, 2, 2, SEQ])
        p_v = ph.ps("p_v", [P, 2, SEQ])
        setup = ph.sem("setup")
        xn_ready, xT_done, xT_ready = (ph.sems(n, 2) for n in ("xn_ready", "xT_done", "xT_ready"))
        qk_ready, v_ready = ph.sems("qk_ready", 2), ph.sems("v_ready", 2)
        hi_ready, rest_ready = ph.sems("hi_ready", 2), ph.sems("rest_ready", 2)
        mid_ready, lo_ready, v_copied = ph.sems("mid_ready", 2), ph.sems("lo_ready", 2), ph.sems("v_copied", 2)
        x_special_ready, k_special_ready = ph.sems("x_special_ready", 2), ph.sems("k_special_ready", 2)
        stored = ph.sems("stored", 2)
        waited = ph.sem("waited")
        n_stores = 3
        block = ph.block()

        @block.vector
        def _(dve):
            dve.memset(strips[:], 1.0)
            if special:
                dve.memset(x_special[:], 0.0)
                for u in range(2):
                    dve.memset(parts[:, u, 1, :, SEQ:KEYS], 0.0)
            dve.tensor_scalar(scaled[:, 0:P], w["q"][:], SCALE, None, ALU.mult)
            dve.tensor_scalar(scaled[:, P:P + 1], w["bq"][:], SCALE, None, ALU.mult).then_inc(setup, 1)
            dve.wait_ge(setup, 1)
            def front(i, u):
                b = 2 * i + u
                wait(dve, xT_done[u], i)
                for t in range(TPB):
                    tile = TPB * b + t
                    last = dve.tensor_scalar(xn[:, u, t, :], src[:, tile, :], mean[:, bass.ds(tile, 1)],
                                             rstd[:, bass.ds(tile, 1)], ALU.subtract, ALU.mult)
                last.then_inc(xn_ready[u], 1)

            def back(i, u):
                wait(dve, stored[u], 16 * n_stores * i)
                for z in range(2):
                    bias = scaled[:, P:P + 1] if z == 0 else w["bk"][:]
                    dve.wait_ge(hi_ready[u], 2 * i + z + 1)
                    wait(dve, lo_ready[u], 2 * i)
                    dve.scalar_tensor_tensor(rest[:, u, z, :], p_qk[:, u, z, :], bias, parts[:, u, z, 0, 0:SEQ],
                                             ALU.add, ALU.subtract).then_inc(rest_ready[u], 1)
                    dve.wait_ge(rest_ready[u], 2 * i + z + 1)
                    dve.tensor_copy(parts[:, u, z, 1, 0:SEQ], rest[:, u, z, :]).then_inc(mid_ready[u], 1)
                dve.wait_ge(v_ready[u], i + 1)
                bias = w["bv"][:].rearrange("p (g j d) -> p g j d", g=HEADS // HG, d=HD)
                if special:
                    dve.tensor_tensor(strips[:, u, :, TPB, :, 0:HD],
                                      p_xT[:, u, 0:P].rearrange("p (g j d) -> p g j d", g=HEADS // HG, d=HD),
                                      bias, ALU.add)
                for g in range(HEADS // HG):
                    last = dve.tensor_tensor(strips[:, u, g, 0:TPB, :, 0:HD],
                                             p_v[:, u, :].rearrange("p (t g j d) -> p g t j d", t=TPB,
                                                                    g=HEADS // HG, d=HD)[:, g],
                                             bias[:, g:g + 1].to_broadcast([P, TPB, HG, HD]), ALU.add)
                last.then_inc(v_copied[u], 1)

            two_ahead(dve, front, back, NB // 2)

        @block.scalar
        def _(act):
            act.wait_ge(setup, 1)
            def front(i, u):
                act.wait_ge(xT_done[u], i + 1)
                wait(act, v_ready[u], i)
                act.activation(xT[:, u, :], p_xT[:, u, :], ACT.Identity, scale=w["gamma"][:],
                               bias=w["beta"][:]).then_inc(xT_ready[u], 1)

            def back(i, u):
                wait(act, stored[u], 16 * n_stores * i)
                for z in range(2):
                    bias = scaled[:, P:P + 1] if z == 0 else w["bk"][:]
                    act.wait_ge(qk_ready[u], 2 * i + z + 1)
                    act.activation(parts[:, u, z, 0, 0:SEQ], p_qk[:, u, z, :], ACT.Identity,
                                   bias=bias).then_inc(hi_ready[u], 1)

            one_ahead(act, front, back, NB // 2)

        @block.gpsimd
        def _(pool):
            pool.wait_ge(setup, 1)

            def step(i, u):
                if special:
                    pool.wait_ge(xT_ready[u], i + 1)
                    wait(pool, v_ready[u], i)
                    pool.sem_inc(waited, 1)
                    c = 0
                    for first, end, stride in SPECIAL:
                        n = len(range(first, end, stride))
                        last = pool.tensor_copy(x_special[:, u, c:c + n], xT[:, u, first:end:stride])
                        c += n
                    last.then_inc(x_special_ready[u], 1)
                wait(pool, stored[u], 16 * n_stores * i)
                for z in range(2):
                    pool.wait_ge(mid_ready[u], 2 * i + z + 1)
                    pool.tensor_tensor(parts[:, u, z, 2, 0:SEQ], rest[:, u, z, :], parts[:, u, z, 1, 0:SEQ],
                                       ALU.subtract).then_inc(lo_ready[u], 1)
                if special:
                    pool.wait_ge(lo_ready[u], 2 * i + 2)
                    pool.sem_inc(waited, 1)
                    c = SEQ
                    for first, end, stride in SPECIAL:
                        n = len(range(first, end, stride))
                        last = pool.tensor_copy(parts[:, u, 1, :, c:c + n], parts[:, u, 1, :, first:end:stride])
                        c += n
                    last.then_inc(k_special_ready[u], 1)

            in_turns(pool, step, NB // 2, 2)

        @block.tensor
        def _(pe):
            pe.wait_ge(setup, 1)
            def front(i, u):
                pe.wait_ge(xn_ready[u], i + 1)
                wait(pe, xT_ready[u], i)
                if special:
                    wait(pe, v_copied[u], i)
                for t in range(TPB):
                    last = pe.transpose(p_xT[:, u, t * P:(t + 1) * P], xn[:, u, t, :], identity[:])
                last.then_inc(xT_done[u], 1)

            def back(i, u):
                pe.wait_ge(xT_ready[u], i + 1)
                wait(pe, rest_ready[u], 2 * i)
                pe.matmul(p_qk[:, u, 0, :], scaled[:, 0:P], xT[:, u, :], start=True, stop=True)\
                    .then_inc(qk_ready[u], 1)
                pe.matmul(p_qk[:, u, 1, :], w["k"][:], xT[:, u, :], start=True, stop=True)\
                    .then_inc(qk_ready[u], 1)
                wait(pe, v_copied[u], i)
                if special:
                    pe.wait_ge(x_special_ready[u], i + 1)
                    pe.matmul(p_xT[:, u, 0:P], x_special[:, u, :], w["v"][:], start=True, stop=True)
                for t in range(TPB):
                    last = pe.matmul(p_v[:, u, t * P:(t + 1) * P], xT[:, u, t * P:(t + 1) * P], w["v"][:],
                                     start=True, stop=True)
                last.then_inc(v_ready[u], 1)

            one_ahead(pe, front, back, NB // 2)

        @block.sync
        def _(sp):
            q_by_seq = q_parts.rearrange("s (b g) r t -> b (g r) s t", g=HG)
            k_by_seq = k_parts.rearrange("s (b g) r t -> b (g r) s t", g=HG)
            v_by_seq = v_strips.rearrange("(b g) p t c -> b p g (t c)", g=HG)
            def step(i, u):
                b = 2 * i + u
                for z, dst, width in ((0, q_by_seq, SEQ), (1, k_by_seq, KW)):
                    if z == 1 and special:
                        sp.wait_ge(k_special_ready[u], i + 1)
                    else:
                        sp.wait_ge(lo_ready[u], 2 * i + z + 1)
                    sp.dma_start(dst[b], parts[:, u, z, :, 0:width]).then_inc(stored[u], 16)
                sp.wait_ge(v_copied[u], i + 1)
                sp.dma_start(v_by_seq[b], strips[:, u].rearrange("p g t j c -> p g (t j c)")).then_inc(stored[u], 16)

            in_turns(sp, step, NB // 2, 2)
            for u in range(2):
                sp.wait_ge(stored[u], 16 * n_stores * (NB // 2))


def attend(nc, name, scratch, ctx_out, identity, identity_bf, masks, penalties):
    q_parts, k_parts, v_strips = scratch
    causal = masks is not None
    KW, VT = (KEYS, TPB + 1) if causal else (SEQ, TPB)

    def fixed(v):
        return causal and v >= HG // 2

    def passes(v):
        if fixed(v):
            return [[(TPB, 0, SEQ)], [(t, t * P, (t + 1) * P) for t in range(TPB)]]
        return [[(t, t * P if causal else 0, SEQ)] for t in range(TPB)]

    PASSES = [len(passes(v)) for v in range(HG)]
    with Phase(nc, name) as ph:
        NBUF, NP = 4, 8
        qs = [ph.sb(f"qs{v}", [P, HG, SEQ], BF16) for v in range(NBUF)]
        ks = [ph.sb(f"ks{v}", [P, HG, KW], BF16) for v in range(NBUF)]
        vs = [ph.sb(f"vs{v}", [P, VT, HG, VW], F32) for v in range(NBUF)]
        neg_max = ph.sb("neg_max", [P, NBUF, HG * TPB], F32)
        max_rest = ph.sb("max_rest", [P, NBUF, HG * TPB], F32)
        max_parts = ph.sb("max_parts", [P, NBUF, P], BF16)
        none = ph.sb("none", [P, HG * TPB], F32)
        max_rows = ph.sb("max_rows", [P, NBUF, P], BF16)
        probs = ph.sb("probs", [P, NP, SEQ], F32)
        ctx_sb = ph.sb("ctx_sb", [P, SEQ], F32)
        den = ph.sb("den", [P, 2, TPB, HG], F32)
        p_max = ph.ps("p_max", [P, 2, 2, SEQ])
        p_sc = ph.ps("p_sc", [P, 2, SEQ])
        p_ctx = ph.ps("p_ctx", [P, SEQ])
        p_tr = ph.ps("p_tr", [P, SEQ])
        p_tr_bf = p_tr[:].bitcast(BF16)
        setup = ph.sem("setup")
        loaded, v_loaded = ph.sems("loaded", NBUF), ph.sems("v_loaded", NBUF)
        rows_cleared = ph.sem("rows_cleared")
        waited = ph.sem("waited")
        max_landed = ph.sems("max_landed", NBUF)
        max_scores, max_done = ph.sem("max_scores"), ph.sem("max_done")
        split_step, split_done = ph.sem("split_step"), ph.sem("split_done")
        rows_ready, rows_copied = ph.sem("rows_ready"), ph.sem("rows_copied")
        scores, exps, products = ph.sem("scores"), ph.sem("exps"), ph.sem("products")
        ctx_copied, ctx_turned, normalised = ph.sem("ctx_copied"), ph.sem("ctx_turned"), ph.sem("normalised")
        norm_step = ph.sem("norm_step")
        LOADS = 2 * len(REPEATS)
        MAXU = 2 * HG
        block = ph.block()

        def at(k, c, m=0):
            return 4 * k + c + m, (c + m) % NBUF, k + (c + m) // NBUF

        def passes_before(k, c, m=0):
            n, v, use = at(k, c, m)
            return sum(PASSES) * use + sum(PASSES[0:v])

        def pipeline(eng, step, first=-3, last=NG):
            for n in range(first, 5):
                step(n // 4, n % 4)
            with eng.Fori(1, NB - 1) as k:
                for c in range(1, 5):
                    step(k, c)
            for n in range(NG - 3, last + 1):
                step(n // 4, n % 4)

        def inside(k, c, m):
            return not isinstance(k, int) or 0 <= 4 * k + c + m < NG

        @block.vector
        def _(dve):
            dve.memset(max_parts[:], 0.0)
            dve.memset(none[:], 0.0)
            for v in range(NBUF):
                dve.memset(qs[v][:], 0.0)
                dve.memset(ks[v][:], 0.0).then_inc(setup, 1)
                dve.wait_ge(setup, 2 * v + 1)
                if causal:
                    for j in range(HG):
                        dve.tensor_copy(qs[v][MROW:P, j, :], penalties[MROW:P, v // 2, 0:SEQ])
                        last = dve.tensor_copy(ks[v][MROW:P, j, :], penalties[MROW:P, v // 2, SEQ:])
                else:
                    last = dve.memset(ks[v][MROW:MROW + 3, :, :], 1.0)
                last.then_inc(setup, 1)

            def reduce_unit(k, c, m):
                n, v, _ = at(k, c, 2)
                j, half = m // 2, m % 2
                col = TPB * j + 2 * half
                dve.wait_ge(max_scores, MAXU * n + m + 1)
                if causal and not fixed(v):
                    for r in range(2):
                        last = dve.tensor_reduce(neg_max[:, v, col + r:col + r + 1],
                                                 p_max[:, m % 2, r, 0:P * (2 * half + r + 1)], AX.X, ALU.max,
                                                 negate=True)
                else:
                    width = P + NSP if causal else SEQ
                    last = dve.tensor_reduce(neg_max[:, v, col:col + 2], p_max[:, m % 2, :, 0:width],
                                             AX.X, ALU.max, negate=True)
                last.then_inc(max_done, 1)

            def normalise(k, c):
                n, v, use = at(k, c, -1)
                turned = p_tr[:].rearrange("p (t j w) -> p t j w", t=TPB, j=HG)
                dve.wait_ge(ctx_turned, n + 1)
                dve.tensor_scalar(den[:, 0], turned[:, :, :, HD], EPS_DEN, None, ALU.max).then_inc(norm_step, 1)
                dve.wait_ge(norm_step, 2 * n + 1)
                dve.reciprocal(den[:, 1], den[:, 0]).then_inc(norm_step, 1)
                dve.wait_ge(norm_step, 2 * n + 2)
                dst = ctx_out[:].rearrange("p (b t) c -> p b t c", t=TPB)[:, use, :, v * HG * HD:(v + 1) * HG * HD]
                dve.tensor_tensor(dst.rearrange("p t (j d) -> p t j d", j=HG), turned[:, :, :, 0:HD],
                                  den[:, 1].rearrange("p t (j o) -> p t j o", o=1)
                                  .to_broadcast([P, TPB, HG, HD]), ALU.mult).then_inc(normalised, 1)

            def step(k, c):
                for m in range(MAXU):
                    if inside(k, c, 2):
                        reduce_unit(k, c, m)
                    if m == 5 and inside(k, c, -1):
                        normalise(k, c)

            pipeline(dve, step, first=-2)

        @block.gpsimd
        def _(pool):
            def step(k, c):
                if inside(k, c, 3):
                    n, v, _ = at(k, c, 3)
                    if isinstance(k, int) and n < NBUF:
                        pool.wait_ge(setup, 2 * v + 2)
                    wait(pool, split_step, 4 * (n - 1))
                    wait(pool, scores, HG * passes_before(k, c))
                    pool.sem_inc(waited, 1)
                    pool.memset(qs[v][MROW:MROW + 3, :, :], 0.0).then_inc(rows_cleared, 1)
                    pool.wait_ge(rows_cleared, n + 1)
                if not inside(k, c, 2):
                    return
                n, v, _ = at(k, c, 2)
                part = [max_parts[:, v, s * HG * TPB:(s + 1) * HG * TPB] for s in range(3)]
                pool.wait_ge(max_done, MAXU * (n + 1))
                pool.tensor_tensor(part[0], neg_max[:, v, :], none[:], ALU.subtract).then_inc(split_step, 1)
                pool.wait_ge(split_step, 4 * n + 1)
                pool.tensor_tensor(max_rest[:, v, :], neg_max[:, v, :], part[0], ALU.subtract)\
                    .then_inc(split_step, 1)
                pool.wait_ge(split_step, 4 * n + 2)
                pool.tensor_tensor(part[1], max_rest[:, v, :], none[:], ALU.subtract).then_inc(split_step, 1)
                pool.wait_ge(split_step, 4 * n + 3)
                pool.tensor_tensor(part[2], max_rest[:, v, :], part[1], ALU.subtract)\
                    .then_inc(split_step, 1)

            pipeline(pool, step, first=-3)

        @block.scalar
        def _(act):
            def copy_rows(k, c):
                n, v, _ = at(k, c, 1)
                act.wait_ge(rows_ready, n + 1)
                act.copy(max_rows[:, v, :], p_tr_bf[:, 0:P]).then_inc(rows_copied, 1)

            def copy_ctx(k, c):
                n, _, _ = at(k, c, -1)
                act.wait_ge(products, passes_before(k, c))
                wait(act, ctx_turned, n)
                act.copy(ctx_sb[:], p_ctx[:]).then_inc(ctx_copied, 1)

            def step(k, c):
                n, v, _ = at(k, c)
                before = passes_before(k, c)
                for s in range(HG * len(passes(v))):
                    if inside(k, c, 0):
                        first, end = passes(v)[s // HG][0][1], passes(v)[s // HG][-1][2]
                        act.wait_ge(scores, HG * before + s + 1)
                        if s % HG == 0:
                            wait(act, products, before + s // HG - 1)
                        act.activation(probs[:, s % NP, first:end], p_sc[:, s % 2, first:end], ACT.Exp)\
                            .then_inc(exps, 1)
                    if s == 5 and inside(k, c, 1):
                        copy_rows(k, c)
                    if s == 4 and inside(k, c, -1):
                        copy_ctx(k, c)

            pipeline(act, step, first=-1)

        @block.tensor
        def _(pe):
            def max_unit(k, c, m):
                n, v, use = at(k, c, 2)
                j, half = m // 2, m % 2
                if m == 0:
                    pe.wait_ge(loaded[v], 16 * LOADS * (use + 1))
                    pe.wait_ge(rows_cleared, n + 1)
                wait(pe, max_done, MAXU * n + m - 1)
                for r in range(2):
                    qt = 2 * half + r
                    bank, q = p_max[:, m % 2, r], qs[v][:, j, qt * P:(qt + 1) * P]
                    if not causal:
                        last = pe.matmul(bank[:, 0:SEQ], q, ks[v][:, j, :], start=True, stop=True)
                    elif fixed(v):
                        pe.matmul(bank[:, 0:P], q, ks[v][:, j, qt * P:(qt + 1) * P], start=True, stop=False)
                        pe.matmul(bank[:, 0:P], identity_bf[:], masks[:, 0, (2 + qt) * P:(3 + qt) * P],
                                  start=False, stop=True)
                        last = pe.matmul(bank[:, P:P + NSP], q, ks[v][:, j, SEQ:SEQ + NSP], start=True, stop=True)
                    else:
                        near = max(0, qt - 1) * P
                        pe.matmul(bank[:, 0:(qt + 1) * P], q, ks[v][:, j, 0:(qt + 1) * P], start=True, stop=False)
                        last = pe.matmul(bank[:, near:(qt + 1) * P], identity_bf[:],
                                         masks[:, 0, near - (qt - 1) * P:2 * P], start=False, stop=True)
                last.then_inc(max_scores, 1)

            def score_unit(k, c, s):
                n, v, use = at(k, c)
                j = s % HG
                if s == 0:
                    pe.wait_ge(max_landed[v], 16 * (use + 1))
                wait(pe, exps, HG * passes_before(k, c) + s - 1)
                for kt, first, end in passes(v)[s // HG]:
                    masked = causal and kt < TPB
                    last = pe.matmul(p_sc[:, s % 2, first:end], ks[v][:, j, kt * P:(kt + 1) * P],
                                     qs[v][:, j, first:end], start=True, stop=not masked)
                    if masked:
                        near = min(end, first + 2 * P)
                        mask = (2 + kt) * P if fixed(v) else 0
                        last = pe.matmul(p_sc[:, s % 2, first:near], identity_bf[:],
                                         masks[:, 1, mask:mask + near - first], start=False, stop=True)
                last.then_inc(scores, 1)

            def value_products(k, c, number, m=0):
                n, v, use = at(k, c, m)
                before = passes_before(k, c, m)
                if number == 0:
                    pe.wait_ge(v_loaded[v], 16 * (use + 1))
                pe.wait_ge(exps, HG * (before + number + 1))
                if number == 0:
                    wait(pe, ctx_copied, n)
                for kt, first, end in passes(v)[number]:
                    for j in range(HG):
                        last = pe.matmul(p_ctx[VW * j:VW * (j + 1), first:end], vs[v][:, kt, j, :],
                                         probs[:, (HG * number + j) % NP, first:end], start=(number == 0),
                                         stop=(number == len(passes(v)) - 1 and end == SEQ))
                last.then_inc(products, 1)

            def turn_rows(k, c):
                n, v, _ = at(k, c, 1)
                pe.wait_ge(split_step, 4 * (n + 1))
                wait(pe, normalised, n - 2)
                pe.transpose(p_tr_bf[:, 0:P], max_parts[:, v, :], identity_bf[:]).then_inc(rows_ready, 1)

            def turn_ctx(k, c):
                n, _, _ = at(k, c, -1)
                pe.wait_ge(ctx_copied, n + 1)
                wait(pe, normalised, n)
                if inside(k, c, 1):
                    pe.wait_ge(rows_copied, n + 3)
                for t in range(TPB):
                    last = pe.transpose(p_tr[:, t * P:(t + 1) * P], ctx_sb[:, t * P:(t + 1) * P], identity[:])
                last.then_inc(ctx_turned, 1)

            def step(k, c):
                number, per_max = len(passes(c % 4)), HG * len(passes(c % 4)) // MAXU
                for s in range(HG * number):
                    if inside(k, c, 0):
                        score_unit(k, c, s)
                    if s == 4 and inside(k, c, 1):
                        turn_rows(k, c)
                    if s % per_max == per_max - 1 and inside(k, c, 2):
                        max_unit(k, c, s // per_max)
                    if s == 1 and inside(k, c, -1):
                        value_products(k, c, len(passes((c - 1) % 4)) - 1, -1)
                    if s in (6, 10, 14) and inside(k, c, 0):
                        value_products(k, c, (s - 6) // 4)
                    if s == min(8, HG * number - 2) and inside(k, c, -1):
                        turn_ctx(k, c)

            pipeline(pe, step, first=-2)

        @block.sync
        def _(sp):
            def move_rows(k, c):
                n, v, _ = at(k, c, 1)
                sp.wait_ge(rows_copied, n + 1)
                sp.dma_start(qs[v][MROW:MROW + 3, :, :].rearrange("p j t -> p (j t)"),
                             max_rows[0:3 * HG * TPB, v, :]).then_inc(max_landed[v], 16)

            def load(k, c):
                n, v, _ = at(k, c, 3)
                if isinstance(k, int) and n < NBUF:
                    sp.wait_ge(setup, 2 * v + 2)
                wait(sp, scores, HG * passes_before(k, c))
                r = 0
                for part, times in enumerate(REPEATS):
                    rows = slice(HD * r, HD * (r + times))
                    sp.dma_start(qs[v][rows, :, :].rearrange("p j t -> p (j t)"),
                                 q_parts[part:part + 1, n].rearrange("s (d j) t -> s d (j t)", d=HD)
                                 .to_broadcast([times, HD, HG * SEQ])).then_inc(loaded[v], 16)
                    sp.dma_start(ks[v][rows, :, :].rearrange("p j t -> p (j t)"),
                                 k_parts[0:times, n].rearrange("s (d j) t -> s d (j t)", d=HD))\
                        .then_inc(loaded[v], 16)
                    r += times

            def load_values(k, c):
                n, v, _ = at(k, c, 3)
                wait(sp, products, passes_before(k, c))
                sp.dma_start(vs[v][:].rearrange("p t j c -> p t (j c)"), v_strips[n]).then_inc(v_loaded[v], 16)

            def step(k, c):
                if inside(k, c, 3):
                    load(k, c)
                if inside(k, c, 1):
                    move_rows(k, c)
                if inside(k, c, 3):
                    load_values(k, c)

            pipeline(sp, step, first=-3)


def attention_out(nc, name, x, ctx_in, w, identity, stats):
    with Phase(nc, name) as ph:
        cx = ph.sb("cx", [P, 2, TPB, D], F32)
        cT = ph.sb("cT", [P, 2, SEQ], F32)
        y = ph.sb("y", [P, 2, TPB, D], F32)
        st = ph.sb("st", [P, 2, TPB, 6], F32)
        p_cT = ph.ps("p_cT", [P, 2, SEQ])
        p_y = ph.ps("p_y", [P, 2, TPB, D])
        copied, turned, cT_ready, y_ready, biased, added, kept, counted = (
            ph.sems(n, 2) for n in ("copied", "turned", "cT_ready", "y_ready", "biased", "added", "kept", "counted"))
        x_by_seq = x[:].rearrange("p (b t) d -> p b t d", t=TPB)
        ctx_by_seq = ctx_in[:].rearrange("p (b t) d -> p b t d", t=TPB)
        block = ph.block()

        @block.tensor
        def _(pe):
            def front(i, u):
                pe.wait_ge(copied[u], i + 1)
                wait(pe, cT_ready[u], i)
                for t in range(TPB):
                    last = pe.transpose(p_cT[:, u, t * P:(t + 1) * P], cx[:, u, t, :], identity[:])
                last.then_inc(turned[u], 1)

            def back(i, u):
                pe.wait_ge(cT_ready[u], i + 1)
                wait(pe, biased[u], i)
                for t in range(TPB):
                    last = pe.matmul(p_y[:, u, t, :], cT[:, u, t * P:(t + 1) * P], w["o"][:], start=True, stop=True)
                last.then_inc(y_ready[u], 1)

            one_ahead(pe, front, back, NB // 2)

        @block.scalar
        def _(act):
            def front(i, u):
                act.wait_ge(turned[u], i + 1)
                wait(act, y_ready[u], i)
                act.copy(cT[:, u, :], p_cT[:, u, :]).then_inc(cT_ready[u], 1)

            def back(i, u):
                act.wait_ge(added[u], i + 1)
                act.copy(x_by_seq[:, 2 * i + u], y[:, u]).then_inc(kept[u], 1)

            one_ahead(act, front, back, NB // 2)

        @block.vector
        def _(dve):
            def front(i, u):
                wait(dve, turned[u], i)
                dve.tensor_copy(cx[:, u], ctx_by_seq[:, 2 * i + u]).then_inc(copied[u], 1)

            def back(i, u):
                b = 2 * i + u
                dve.wait_ge(y_ready[u], i + 1)
                wait(dve, kept[u], i)
                dve.tensor_tensor(y[:, u], p_y[:, u],
                                  w["bo"][:].rearrange("p (o d) -> p o d", o=1).to_broadcast([P, TPB, D]),
                                  ALU.add).then_inc(biased[u], 1)
                dve.wait_ge(biased[u], i + 1)
                dve.tensor_tensor(y[:, u], x_by_seq[:, b], y[:, u], ALU.add).then_inc(added[u], 1)
                dve.wait_ge(added[u], i + 1)
                wait(dve, counted[u], 2 * i)
                for t in range(TPB):
                    last = dve.bn_stats(st[:, u, t, :], y[:, u, t, :])
                last.then_inc(counted[u], 1)
                dve.wait_ge(counted[u], 2 * i + 1)
                dve.tensor_copy(stats[:].rearrange("p (b t) s -> p b t s", t=TPB)[:, b], st[:, u])\
                   .then_inc(counted[u], 1)

            two_ahead(dve, front, back, NB // 2)


def route(nc, name, x, mean, rstd, w, identity, positions, weights, slot_group):
    NS = RG + EXPERTS
    with Phase(nc, name) as ph:
        xn = ph.sb("xn", [P, 2, TPB, D], F32)
        xT = ph.sb("xT", [P, 2, SEQ], F32)
        logits = ph.sb("logits", [P, NT, NS], F32)
        sig = ph.sb("sig", [P, NT, NS], F32)
        top = ph.sb("top", [P, NT], F32)
        top_w = ph.sb("top_w", [P, 2, NT], F32)
        taken = ph.sb("taken", [P, NT], F32)
        equal = ph.sb("equal", [P, NT, RG], F32)
        onehot = ph.sb("onehot", [P, NT, RG], F32)
        onehot_bf = ph.sb("onehot_bf", [P, NT, RG], BF16)
        chosen = ph.sb("chosen", [P, NT, RG, EPG], F32)
        micro = ph.sb("micro", [P, NT, EPG], F32)
        micro_sum = ph.sb("micro_sum", [P, NT], F32)
        counts = ph.sb("counts", [P, 3, NT, RG], F32)
        padded = ph.sb("padded", [P, RG], I32)
        starts = ph.sb("starts", [P, 2, RG], F32)
        place = ph.sb("place", [P, NT, RG], F32)
        place_sum = ph.sb("place_sum", [P, NT], F32)
        slot_f = ph.sb("slot_f", [P, 2, SLOTS], F32)
        p_xT = ph.ps("p_xT", [P, 2, SEQ])
        p_log = ph.ps("p_log", [P, 2, SEQ])
        p_rank = ph.ps("p_rank", [P, 2, SEQ])
        xn_ready, turned, xT_ready, log_ready, log_copied = (
            ph.sems(n, 2) for n in ("xn_ready", "turned", "xT_ready", "log_ready", "log_copied"))
        sig_ready, onehot_ready, rank_ready, dve_step = (
            ph.sem(n) for n in ("sig_ready", "onehot_ready", "rank_ready", "dve_step"))
        block = ph.block()

        @block.tensor
        def _(pe):
            def front(i, u):
                pe.wait_ge(xn_ready[u], i + 1)
                wait(pe, xT_ready[u], i)
                for t in range(TPB):
                    last = pe.transpose(p_xT[:, u, t * P:(t + 1) * P], xn[:, u, t, :], identity[:])
                last.then_inc(turned[u], 1)

            def back(i, u):
                pe.wait_ge(xT_ready[u], i + 1)
                wait(pe, log_copied[u], i)
                for t in range(TPB):
                    last = pe.matmul(p_log[:, u, NS * t:NS * (t + 1)], xT[:, u, t * P:(t + 1) * P],
                                     w["router"][:], start=True, stop=True)
                last.then_inc(log_ready[u], 1)

            one_ahead(pe, front, back, NB // 2)
            pe.wait_ge(onehot_ready, 1)
            flat = onehot_bf[:].rearrange("p t g -> p (t g)")
            pe.matmul(p_rank[:, 0, 0:NT * RG], w["before"][:], flat, start=True, stop=True)
            pe.matmul(p_rank[:, 1, 0:NT * RG], w["ones"][:], flat, start=True, stop=True).then_inc(rank_ready, 1)

        @block.scalar
        def _(act):
            def step(i, u):
                act.wait_ge(turned[u], i + 1)
                wait(act, log_ready[u], i)
                act.copy(xT[:, u, :], p_xT[:, u, :]).then_inc(xT_ready[u], 1)

            in_turns(act, step, NB // 2, 2)
            for u in range(2):
                act.wait_ge(log_copied[u], NB // 2)
            act.activation(sig[:], logits[:], ACT.Sigmoid).then_inc(sig_ready, 1)

        @block.vector
        def _(dve):
            def front(i, u):
                b = 2 * i + u
                wait(dve, turned[u], i)
                for t in range(TPB):
                    tile = TPB * b + t
                    last = dve.tensor_scalar(xn[:, u, t, :], x[:, tile, :], mean[:, bass.ds(tile, 1)],
                                             rstd[:, bass.ds(tile, 1)], ALU.subtract, ALU.mult)
                last.then_inc(xn_ready[u], 1)

            def back(i, u):
                b = 2 * i + u
                dve.wait_ge(log_ready[u], i + 1)
                dve.tensor_copy(logits[:].rearrange("p (b t) n -> p b (t n)", t=TPB)[:, b],
                                p_log[:, u, 0:TPB * NS]).then_inc(log_copied[u], 1)

            two_ahead(dve, front, back, NB // 2)
            dve.wait_ge(sig_ready, 1)
            done = [0]

            def then(instruction):
                done[0] += 1
                instruction.then_inc(dve_step, 1)
                dve.wait_ge(dve_step, done[0])

            then(dve.tensor_reduce(top[:], sig[:, :, 0:RG], AX.X, ALU.max))
            then(dve.tensor_tensor(equal[:], sig[:, :, 0:RG],
                                   top[:].rearrange("p (t o) -> p t o", o=1).to_broadcast([P, NT, RG]), ALU.is_equal))
            dve.tensor_copy(onehot[:, :, 0], equal[:, :, 0])
            then(dve.tensor_copy(taken[:], equal[:, :, 0]))
            for g in range(1, RG):
                dve.tensor_tensor(onehot[:, :, g], equal[:, :, g], taken[:], ALU.is_gt)
                then(dve.tensor_tensor(taken[:], equal[:, :, g], taken[:], ALU.max))
            dve.tensor_copy(onehot_bf[:], onehot[:]).then_inc(onehot_ready, 1)
            then(dve.tensor_scalar(top_w[:, 0], top[:], EPS_TOPK, None, ALU.add))
            then(dve.reciprocal(top_w[:, 1], top_w[:, 0]))
            then(dve.tensor_tensor(top_w[:, 0], top[:], top_w[:, 1], ALU.mult))
            then(dve.tensor_tensor(chosen[:], sig[:, :, RG:NS].rearrange("p t (g e) -> p t g e", g=RG),
                                   onehot[:].rearrange("p t (g o) -> p t g o", o=1).to_broadcast([P, NT, RG, EPG]),
                                   ALU.mult))
            then(dve.tensor_reduce(micro[:], chosen[:].rearrange("p t g e -> p t e g"), AX.X, ALU.add))
            then(dve.tensor_tensor(micro_sum[:], micro[:, :, 0], micro[:, :, 1], ALU.add))
            then(dve.tensor_scalar(micro_sum[:], micro_sum[:], EPS_TOPK, None, ALU.add))
            then(dve.reciprocal(top_w[:, 1], micro_sum[:]))
            for e in range(EPG):
                then(dve.tensor_tensor(micro[:, :, e], micro[:, :, e], top_w[:, 1], ALU.mult))
                then(dve.tensor_tensor(weights[:, :, e], micro[:, :, e], top_w[:, 0], ALU.mult))
            dve.wait_ge(rank_ready, 1)
            totals = p_rank[:, 1, 0:NT * RG].rearrange("p (t g) -> p t g", g=RG)
            then(dve.tensor_copy(counts[:, 0], totals))
            cur, shift = 0, 1
            while shift < NT:
                dve.tensor_copy(counts[:, 1 - cur, 0:shift], counts[:, cur, 0:shift])
                then(dve.tensor_tensor(counts[:, 1 - cur, shift:NT], counts[:, cur, shift:NT],
                                       counts[:, cur, 0:NT - shift], ALU.add))
                cur, shift = 1 - cur, 2 * shift
            running = counts[:, cur]
            then(dve.tensor_scalar(padded[:], running[:, NT - 1, :], float(P - 1), None, ALU.add))
            then(dve.tensor_scalar(padded[:], padded[:], 7, 7, ALU.logical_shift_right, ALU.logical_shift_left))
            then(dve.tensor_copy(starts[:, 0], padded[:]))
            then(dve.memset(starts[:, 1, 0:1], 0.0))
            for g in range(1, RG):
                then(dve.tensor_tensor(starts[:, 1, g:g + 1], starts[:, 1, g - 1:g], starts[:, 0, g - 1:g], ALU.add))
            then(dve.tensor_tensor(place[:], running, totals, ALU.subtract))
            then(dve.tensor_tensor(place[:], place[:], p_rank[:, 0, 0:NT * RG].rearrange("p (t g) -> p t g", g=RG),
                                   ALU.add))
            then(dve.tensor_tensor(place[:], place[:],
                                   starts[:, 1].rearrange("p (o g) -> p o g", o=1).to_broadcast([P, NT, RG]), ALU.add))
            then(dve.tensor_tensor(place[:], place[:], onehot[:], ALU.mult))
            then(dve.tensor_reduce(place_sum[:], place[:], AX.X, ALU.add))
            then(dve.tensor_copy(positions[:], place_sum[:]))
            then(dve.tensor_scalar(slot_f[:, 0], w["slot_rows"][:], starts[:, 1, 1:2], None, ALU.is_ge))
            for g in range(2, RG):
                then(dve.tensor_scalar(slot_f[:, 1], w["slot_rows"][:], starts[:, 1, g:g + 1], None, ALU.is_ge))
                then(dve.tensor_tensor(slot_f[:, 0], slot_f[:, 0], slot_f[:, 1], ALU.add))
            then(dve.tensor_copy(slot_group[:], slot_f[0:1, 0]))


def scatter_rows(nc, name, x, mean, rstd, positions, weights, sorted_rows, clear):
    with Phase(nc, name) as ph:
        NR = 4
        zero = ph.sb("zero", [P, SLOTS * ROW // 4], F32)
        rows = [ph.sb(f"rows{u}", [P, ROW], F32) for u in range(NR)]
        index = [ph.sb(f"index{u}", [P, 1], U32) for u in range(NR)]
        zeroed, cleared, begun = ph.sem("zeroed"), ph.sem("cleared"), ph.sem("begun")
        ready, written = ph.sems("ready", NR), ph.software_sems(NR)
        block = ph.block()

        if clear:
            @block.sync
            def _(sp):
                sp.wait_ge(zeroed, 1)
                flat = sorted_rows.rearrange("(q p s) c -> q p (s c)", q=4, p=P)
                for q in range(4):
                    sp.dma_start(flat[q], zero[:]).then_inc(cleared, 16)

        @block.vector
        def _(dve):
            if clear:
                dve.memset(zero[:], 0.0).then_inc(zeroed, 1)
            def step(i, u):
                t = NR * i + u
                wait(dve, written[u], 16 * i)
                dve.tensor_scalar(rows[u][:, 0:D], x[:, t, :], mean[:, bass.ds(t, 1)], rstd[:, bass.ds(t, 1)],
                                  ALU.subtract, ALU.mult)
                dve.tensor_copy(rows[u][:, D:ROW], weights[:, t, :])
                dve.tensor_copy(index[u][:], positions[:, bass.ds(t, 1)]).then_inc(ready[u], 1)

            in_turns(dve, step, NT // NR, NR)

        @block.gpsimd
        def _(pool):
            if clear:
                pool.wait_ge(cleared, 16 * 4)
            def step(i, u):
                pool.wait_ge(ready[u], i + 1)
                pool.sem_inc(begun, 1)
                pool.indirect_dma_start(sorted_rows, bass.IndirectOffsetOnAxis(ap=index[u][:, 0:1], axis=0),
                                        rows[u][:], None).then_inc(written[u], 16)

            in_turns(pool, step, NT // NR, NR)
            for u in range(NR):
                pool.wait_ge(written[u], 16 * (NT // NR))


def experts(nc, name, sorted_rows, sorted_out, slot_group, w, identity):
    with Phase(nc, name) as ph:
        NR = 4
        rows = ph.sb("rows", [P, NR, ROW], F32)
        xT = ph.sb("xT", [P, 2, P], F32)
        act_g = ph.sb("act_g", [P, 2, EPG, FF], F32)
        hidden = ph.sb("hidden", [P, 2, EPG, FF], F32)
        hT = ph.sb("hT", [P, 2, DNC * P], F32)
        y = ph.sb("y", [P, 2, D], F32)
        p_gu = ph.ps("p_gu", [P, 2, EPG, 2 * FF])
        p_hT = ph.ps("p_hT", [P, SEQ])
        p_xT = ph.ps("p_xT", [P, 2, SEQ])
        p_y = ph.ps("p_y", [P, SEQ])
        loaded, stored = ph.sems("loaded", NR), ph.software_sems(2)
        x_turned, xT_ready, gu_ready, silu_ready = (ph.sem(n) for n in ("x_turned", "xT_ready", "gu_ready", "silu_ready"))
        hidden_ready, h_turned, hT_ready, y_ready, y_copied = (
            ph.sem(n) for n in ("hidden_ready", "h_turned", "hT_ready", "y_ready", "y_copied"))
        rows_by_slot = sorted_rows.rearrange("(s p) c -> s p c", p=P)
        out_by_slot = sorted_out.rearrange("(s p) c -> s p c", p=P)
        block = ph.block()

        def pipeline(eng, body):
            body(0)
            with eng.Fori(1, SLOTS // NR - 1) as i:
                body(i)
            body(SLOTS // NR - 1)

        def steps(step):
            def body(i):
                for u in range(NR + 1 if isinstance(i, int) and i == SLOTS // NR - 1 else NR):
                    step(i, u)
            return body

        def first(s):
            return isinstance(s, int) and s == 0

        def last_slot(s):
            return isinstance(s, int) and s == SLOTS - 1

        def past(s):
            return isinstance(s, int) and s == SLOTS

        @block.sync
        def _(sp):
            def step(i, u):
                s = NR * i + u
                if past(s):
                    return
                wait(sp, hidden_ready, s - NR + 1)
                wait(sp, x_turned, s - NR + 1)
                sp.dma_start(rows[:, u, :], rows_by_slot[s]).then_inc(loaded[u], 16)

            pipeline(sp, steps(step))

        @block.scalar
        def _(act):
            def step(i, u):
                s = NR * i + u
                if not first(s):
                    act.wait_ge(h_turned, s)
                    wait(act, y_ready, s - 2)
                    act.copy(hT[:, (u - 1) % 2, :], p_hT[:]).then_inc(hT_ready, 1)
                if not past(s):
                    act.wait_ge(gu_ready, s + 1)
                    wait(act, hidden_ready, s - 1)
                    act.activation(act_g[:, u % 2], p_gu[:, u % 2, :, 0:FF], ACT.Silu).then_inc(silu_ready, 1)

            pipeline(act, steps(step))

        @block.vector
        def _(dve):
            def copy_xT(s, v):
                dve.wait_ge(x_turned, s + 1)
                wait(dve, gu_ready, s - 1)
                dve.tensor_copy(xT[:, v, :], p_xT[:, v, 0:P]).then_inc(xT_ready, 1)

            def step(i, u):
                s = NR * i + u
                if first(s):
                    copy_xT(0, 0)
                if not (past(s) or last_slot(s)):
                    copy_xT(s + 1, (u + 1) % 2)
                if not past(s):
                    dve.wait_ge(silu_ready, s + 1)
                    wait(dve, h_turned, s - 1)
                    for e in range(EPG):
                        last = dve.scalar_tensor_tensor(hidden[:, u % 2, e, :], act_g[:, u % 2, e, :],
                                                        rows[:, u, D + e:D + e + 1],
                                                        p_gu[:, u % 2, e, FF:2 * FF], ALU.mult, ALU.mult)
                    last.then_inc(hidden_ready, 1)
                if not first(s):
                    v = (u - 1) % 2
                    dve.wait_ge(y_ready, s)
                    wait(dve, stored[v], 16 * (NR // 2 * i + (u - 1) // 2))
                    dve.tensor_copy(y[:, v, :], p_y[:, 0:D]).then_inc(y_copied, 1)

            pipeline(dve, steps(step))

        @block.gpsimd
        def _(pool):
            def step(i, u):
                s = NR * i + u
                if not first(s):
                    pool.wait_ge(y_copied, s)
                    pool.dma_start(out_by_slot[s - 1], y[:, (u - 1) % 2, :]).then_inc(stored[(u - 1) % 2], 16)

            pipeline(pool, steps(step))
            for u in range(2):
                pool.wait_ge(stored[u], 16 * (SLOTS // 2))

        @block.tensor
        def _(pe):
            gu = w["gate_up"][:].rearrange("p (g e) f -> p g e f", g=RG)
            dn = w["down"][:].rearrange("p (g c) d -> p g c d", g=RG)

            def turn_x(s, v, i):
                pe.wait_ge(loaded[v], 16 * (i + 1))
                wait(pe, xT_ready, s - 1)
                pe.transpose(p_xT[:, v % 2, 0:P], rows[:, v, 0:D], identity[:]).then_inc(x_turned, 1)

            def gate_up(group, u, e):
                last = pe.matmul(p_gu[:, u % 2, e, :], xT[:, u % 2, :], gu[:, group, e, :], start=True, stop=True)
                if e == EPG - 1:
                    last.then_inc(gu_ready, 1)

            def body(i):
                ends = isinstance(i, int) and i == SLOTS // NR - 1
                group = {u: pe.value_load(slot_group[0:1, bass.ds(NR * i + u, 1)], min_val=0, max_val=RG - 1)
                         for u in range(0 if first(i) else -1, NR)}
                for u in range(NR + 1 if ends else NR):
                    s = NR * i + u
                    if first(s):
                        turn_x(0, 0, 0)
                    if not past(s):
                        pe.wait_ge(xT_ready, s + 1)
                        wait(pe, hidden_ready, s - 1)
                        gate_up(group[u], u, 0)
                    if not first(s):
                        pe.wait_ge(hidden_ready, s)
                        wait(pe, hT_ready, s - 1)
                        for c in range(DNC):
                            last = pe.transpose(p_hT[:, c * P:(c + 1) * P],
                                                hidden[:, (u - 1) % 2].rearrange("p e f -> p (e f)")[:, c * P:(c + 1) * P],
                                                identity[:])
                        last.then_inc(h_turned, 1)
                    if not (past(s) or last_slot(s)):
                        turn_x(s + 1, (u + 1) % NR, i + (u + 1) // NR)
                    if not past(s):
                        gate_up(group[u], u, 1)
                    if not first(s):
                        pe.wait_ge(hT_ready, s)
                        wait(pe, y_copied, s - 1)
                        for c in range(DNC):
                            last = pe.matmul(p_y[:, 0:D], hT[:, (u - 1) % 2, c * P:(c + 1) * P],
                                             dn[:, group[u - 1], c, :], start=(c == 0), stop=(c == DNC - 1))
                        last.then_inc(y_ready, 1)

            pipeline(pe, body)


def gather_rows(nc, name, x, positions, sorted_out, stats):
    with Phase(nc, name) as ph:
        NR = 4
        rows = [ph.sb(f"rows{u}", [P, D], F32) for u in range(NR)]
        index = [ph.sb(f"index{u}", [P, 1], U32) for u in range(NR)]
        st = ph.sb("st", [P, NR, 6], F32)
        indexed, fetched, added = ph.sems("indexed", NR), ph.software_sems(NR), ph.sems("added", NR)
        counted, kept = ph.sems("counted", NR), ph.sems("kept", NR)
        begun = ph.sem("begun")
        block = ph.block()

        @block.scalar
        def _(act):
            def name_rows(i, u):
                wait(act, fetched[u], 16 * i)
                act.copy(index[u][:], positions[:, bass.ds(NR * i + u, 1)]).then_inc(indexed[u], 1)

            def keep(i, u):
                act.wait_ge(added[u], i + 1)
                act.copy(x[:, NR * i + u, :], rows[u][:])
                act.wait_ge(counted[u], i + 1)
                act.copy(stats[:, NR * i + u, :], st[:, u, :]).then_inc(kept[u], 1)

            for u in range(NR):
                name_rows(0, u)
            with act.Fori(1, NT // NR) as i:
                for u in range(NR):
                    name_rows(i, u)
                    keep(i - 1, u)
            for u in range(NR):
                keep(NT // NR - 1, u)

        @block.gpsimd
        def _(pool):
            def step(i, u):
                pool.wait_ge(indexed[u], i + 1)
                wait(pool, kept[u], i)
                pool.sem_inc(begun, 1)
                pool.indirect_dma_start(rows[u][:], None, sorted_out,
                                        bass.IndirectOffsetOnAxis(ap=index[u][:, 0:1], axis=0))\
                    .then_inc(fetched[u], 16)

            in_turns(pool, step, NT // NR, NR)

        @block.vector
        def _(dve):
            def step(i, u):
                dve.wait_ge(fetched[u], 16 * (i + 1))
                dve.tensor_tensor(rows[u][:], x[:, NR * i + u, :], rows[u][:], ALU.add).then_inc(added[u], 1)
                dve.wait_ge(added[u], i + 1)
                dve.bn_stats(st[:, u, :], rows[u][:]).then_inc(counted[u], 1)

            in_turns(dve, step, NT // NR, NR)


def build(nc, a, out):
    with Phase(nc, "all") as ph:
        Phase.own_sems = [ph.sem(f"software_dma{i}") for i in range(2 * (4 + 2 + 4))]
        x = ph.sb("x", [P, NT, D], F32)
        stats = ph.sb("stats", [P, NT, 6], F32)
        mean, rstd = ph.sb("mean", [P, NT], F32), ph.sb("rstd", [P, NT], F32)
        before = ph.sb("before_f", [P, P], F32)
        identity, identity_bf = ph.sb("identity", [P, P], F32), ph.sb("identity_bf", [P, P], BF16)
        positions = ph.sb("positions", [P, NT], U32)
        weights = ph.sb("weights", [P, NT, EPG], F32)
        slot_group = ph.sb("slot_group", [1, SLOTS], I32)
        ffn = {"gate_up": ph.sb("gate_up", [P, EXPERTS, 2 * FF], F32), "down": ph.sb("down", [P, EXPERTS * 2, D], F32),
               "router": ph.sb("router", [P, RG + EXPERTS], F32), "before": ph.sb("before", [P, P], BF16),
               "ones": ph.sb("ones", [P, P], BF16), "slot_rows": ph.sb("slot_rows", [P, SLOTS], F32)}
        wa, wb = ({k: ph.sb(f"{n}_{k}", [P, P], F32) for k in ("q", "k", "v", "o", "bv", "bo")} |
                  {k: ph.sb(f"{n}_{k}", [P, 1], F32) for k in ("bq", "bk", "gamma", "beta")} for n in "ab")
        q_parts = nc.dram_tensor("q_parts", [3, NG, HG * HD, SEQ], BF16, kind="Internal").ap()
        sorted_rows = nc.dram_tensor("sorted_rows", [SLOTS * P, ROW], F32, kind="Internal").ap()
        sorted_out = nc.dram_tensor("sorted_out", [SLOTS * P, D], F32, kind="Internal").ap()
        scratch = [(q_parts, nc.dram_tensor(f"k_parts{z}", [3, NG, HG * HD, SEQ + z * P], BF16, kind="Internal").ap(),
                    nc.dram_tensor(f"v_strips{z}", [NG, P, TPB + z, HG * VW], F32, kind="Internal").ap())
                   for z in range(2)]

        def column(v):
            return v.rearrange("(d o) -> d o", o=1)

        def on_all_rows(v):
            return v.rearrange("(o d) -> o d", o=1).to_broadcast([P, v.shape[0]])

        x_in = a["L0_attn_a_x"].rearrange("b (t p) d -> p (b t) d", p=P)
        loads = [(x[:, NT // 4 * q:NT // 4 * (q + 1), :], x_in[:, NT // 4 * q:NT // 4 * (q + 1), :]) for q in range(4)]
        loads += [(wa[k][:], a["L0_attn_a_W_qkv"][:, i * D:(i + 1) * D]) for i, k in enumerate("qkv")]
        bias = a["L0_attn_a_b_qkv"]
        loads += [(wa["o"][:], a["L0_attn_a_W_proj"]), (wa["bo"][:], on_all_rows(a["L0_attn_a_b_proj"])),
                  (wa["bq"][:], column(bias[0:D])), (wa["bk"][:], column(bias[D:2 * D])),
                  (wa["bv"][:], on_all_rows(bias[2 * D:3 * D])),
                  (wa["gamma"][:], column(a["L0_attn_a_ln_gamma"])), (wa["beta"][:], column(a["L0_attn_a_ln_beta"]))]
        loads += [(wb[k][:], a[n]) for k, n in (("q", "WqT"), ("k", "WkT"), ("v", "WvT"), ("o", "WoT"))]
        loads += [(ffn["gate_up"][:, :, 0:FF], a["L0_ffn_gate_w"].rearrange("n d f -> d n f")),
                  (ffn["gate_up"][:, :, FF:2 * FF], a["L0_ffn_up_w"].rearrange("n d f -> d n f")),
                  (ffn["down"][:], a["L0_ffn_down_w"].rearrange("n (h p) d -> p (n h) d", p=P)),
                  (ffn["router"][:, 0:RG], a["L0_ffn_macro_w"]),
                  (ffn["router"][:, RG:].rearrange("p (g e) -> p g e", g=RG),
                   a["L0_ffn_micro_w"].rearrange("g d e -> d g e")),
                  (identity[:], a["identity"]), (before[:], a["before"]),
                  (ffn["slot_rows"][:], a["slot_rows"])]
        with Phase(nc, "load") as ld:
            x_landed, weights_landed = ld.sems("x_landed", 4), ld.sem("weights_landed")
            block = ld.block()

            @block.sync
            def _(sp):
                for q, (dst, src) in enumerate(loads[0:4]):
                    sp.dma_start(dst, src).then_inc(x_landed[q], 16)
                for dst, src in loads[4:]:
                    sp.dma_start(dst, src).then_inc(weights_landed, 16)
                sp.wait_ge(weights_landed, 16 * len(loads[4:]))

            @block.vector
            def _(dve):
                for q in range(4):
                    dve.wait_ge(x_landed[q], 16)
                    for t in range(NT // 4 * q, NT // 4 * (q + 1)):
                        dve.bn_stats(stats[:, t, :], x[:, t, :])

        with Phase(nc, "const") as c:
            block = c.block()

            @block.vector
            def _(dve):
                dve.tensor_copy(identity_bf[:], identity[:])
                dve.tensor_copy(ffn["before"][:], before[:])
                dve.memset(ffn["ones"][:], 1.0)
                for k in ("bv", "bo", "bq", "bk", "beta"):
                    dve.memset(wb[k][:], 0.0)
                dve.memset(wb["gamma"][:], 1.0)

        def mixture(n, clear):
            finish_stats(nc, f"{n}s", stats, mean, rstd, False)
            route(nc, f"{n}r", x, mean, rstd, ffn, identity, positions, weights, slot_group)
            scatter_rows(nc, f"{n}c", x, mean, rstd, positions, weights, sorted_rows, clear)
            experts(nc, f"{n}e", sorted_rows, sorted_out, slot_group, ffn, identity)
            gather_rows(nc, f"{n}g", x, positions, sorted_out, stats)

        def attention(n, w, twice, masks, penalties):
            special = masks is not None
            with Phase(nc, n) as p2:
                ctx = p2.sb("ctx", [P, NT, D], F32)
                finish_stats(nc, f"{n}s", stats, mean, rstd, twice)
                project(nc, f"{n}p", x, mean, rstd, w, scratch[special], identity, special)
                attend(nc, f"{n}a", scratch[special], ctx, identity, identity_bf, masks, penalties)
                attention_out(nc, f"{n}o", x, ctx, w, identity, stats)

        attention("A", wa, True, None, None)
        mixture("F", True)
        with Phase(nc, "m") as mk:
            masks = mk.sb("masks", [P, 2, (2 + TPB) * P], BF16)
            penalties = mk.sb("penalties", [P, 2, SEQ + KEYS], BF16)
            with Phase(nc, "mf") as mf:
                masks_f = mf.sb("masks_f", [P, 2, (2 + TPB) * P], F32)
                penalties_f = mf.sb("penalties_f", [P, 2, SEQ + KEYS], F32)
                masks_landed, penalties_landed = mf.sem("masks_landed"), mf.sem("penalties_landed")
                block = mf.block()

                @block.sync
                def _(sp):
                    sp.dma_start(masks_f[:], a["masks"]).then_inc(masks_landed, 16)
                    sp.dma_start(penalties_f[:], a["penalties"]).then_inc(penalties_landed, 16)

                @block.vector
                def _(dve):
                    dve.wait_ge(masks_landed, 16)
                    dve.tensor_copy(masks[:], masks_f[:])
                    dve.wait_ge(penalties_landed, 16)
                    dve.tensor_copy(penalties[:], penalties_f[:])
            attention("B", wb, False, masks, penalties)
        mixture("G", False)
        with Phase(nc, "out") as o:
            stored = o.sem("stored")
            block = o.block()

            @block.sync
            def _(sp):
                out_v = out.rearrange("b (t p) d -> p (b t) d", p=P)
                for q in range(4):
                    sp.dma_start(out_v[:, NT // 4 * q:NT // 4 * (q + 1), :], x[:, NT // 4 * q:NT // 4 * (q + 1), :]).then_inc(stored, 16)
                sp.wait_ge(stored, 16 * 4)


def shape_constants():
    import numpy as np

    never = -1e38
    i, j = np.arange(SEQ)[:, None], np.arange(SEQ)[None, :]
    causal = j <= i
    seen = [causal & ((i - j < STRIDE) | (j % STRIDE == i % STRIDE)),
            causal & ((j // STRIDE == i // STRIDE) | (j % STRIDE >= STRIDE - 1))]
    strided, fixed = (np.where(ok, 0.0, never).astype(np.float32) for ok in seen)
    masks = np.zeros((P, 2, (2 + TPB) * P), np.float32)
    masks[:, 0, 0:2 * P] = strided[P:2 * P, 0:2 * P]
    masks[:, 1, 0:2 * P] = strided[0:2 * P, 0:P].T
    for t in range(TPB):
        tile = fixed[t * P:(t + 1) * P, t * P:(t + 1) * P]
        masks[:, 0, (2 + t) * P:(3 + t) * P] = tile
        masks[:, 1, (2 + t) * P:(3 + t) * P] = tile.T

    penalties = np.zeros((P, 2, SEQ + KEYS), np.float32)
    penalties[MROW:MROW + 3, :, SEQ:] = 1.0
    token = np.arange(SEQ)
    row = MROW + 3
    for kt in range(TPB - 2):
        for residue in range(STRIDE):
            penalties[row, 0, 0:SEQ] = (token % STRIDE == residue) & (token // P >= kt + 2)
            penalties[row, 0, SEQ:2 * SEQ] = np.where((token % STRIDE != residue) & (token // P == kt), never, 0.0)
            row += 1
    assert row <= P
    row = MROW + 3
    special = np.full(P, SEQ)
    special[0:NSP] = SPECIAL_KEYS
    for tile, blk in sorted({(t // P, t // STRIDE) for t in range(SEQ)}):
        penalties[row, 1, 0:SEQ] = (token // P == tile) & (token // STRIDE == blk)
        ok = (special // P < tile) & ((special // STRIDE == blk) | (special % STRIDE == STRIDE - 1))
        penalties[row, 1, 2 * SEQ:] = np.where(ok, 0.0, never)
        row += 1
    assert row <= P
    return {"identity": np.eye(P, dtype=np.float32), "before": np.triu(np.ones((P, P), np.float32), 1),
            "slot_rows": np.tile(np.arange(SLOTS, dtype=np.float32) * P, (P, 1)),
            "masks": masks, "penalties": penalties}


def by_dimension(columns):
    import numpy as np

    shape = columns.shape[:-1]
    return np.ascontiguousarray(columns.reshape(*shape, HEADS // HG, HG, HD).swapaxes(-1, -2).reshape(*shape, D))


def kernel(**inputs):
    import numpy as _np
    import concourse.bacc as _bacc
    from concourse import mybir as _mybir
    from concourse.bass_utils import run_bass_kernel_spmd as _run

    nc = _bacc.Bacc("TRN2", target_bir_lowering=False, num_devices=1)
    given = {}
    for name, value in inputs.items():
        value = _np.asarray(value)
        if name in ("L0_attn_b_Wq", "L0_attn_b_Wk"):
            given[name[-2:] + "T"] = by_dimension(value.T)
        elif name in ("L0_attn_b_Wv", "L0_attn_b_Wo"):
            given[name[-2:] + "T"] = _np.ascontiguousarray(value.T)
        elif name in ("L0_attn_a_W_qkv", "L0_attn_a_b_qkv"):
            given[name] = _np.concatenate([by_dimension(value[..., 0:D]), by_dimension(value[..., D:2 * D]),
                                           value[..., 2 * D:]], axis=-1)
        else:
            given[name] = _np.ascontiguousarray(value)
    given.update(shape_constants())
    arrays, args = {}, {}
    for name, v in given.items():
        arrays[f"in_{name}"] = v
        args[name] = nc.dram_tensor(f"in_{name}", v.shape, _mybir.dt.from_np(v.dtype), kind="ExternalInput").ap()
    out = nc.dram_tensor("out_0", [NB, SEQ, D], _mybir.dt.float32, kind="ExternalOutput").ap()
    build(nc, args, out)
    r = _run(nc, [arrays], core_ids=[0])
    return r.results[0]["out_0"]
```
